# Optimizing a Trainium2 kernel written in Bass

```python
import numpy as np
import jax
import jax.numpy as jnp

def _softmax(x, axis=-1):
    return jax.nn.softmax(x, axis=axis)

def _gelu(x):
    return jax.nn.gelu(x, approximate=True)

def _silu(x):
    return jax.nn.silu(x)

def _sigmoid(x):
    return jax.nn.sigmoid(x)

def _layernorm(x, axis=-1, eps=1e-05):
    m = jnp.mean(x, axis=axis, keepdims=True)
    v = jnp.var(x, axis=axis, keepdims=True)
    return (x - m) / jnp.sqrt(v + eps)

def _scatter_add(tgt, idx, src, axis=0):
    return tgt.at[idx].add(src)

def _segment_sum(src, seg, n):
    return jax.ops.segment_sum(src, seg, n)
kernel_name = 'mk_seq_preln_d2_jaxref_r8_92dc67'

def setup_inputs(seed: int=0):
    np.random.seed(seed)
    _w = jnp.asarray

    def _L0_attn_setup():
        import jax, jax.numpy as jnp
        import numpy as np
        B, S, DIN, DIM = (1, 512, 128, 128)
        NH, NKV = (16, 4)
        HD = DIM // NH
        GS = NH // NKV
        key = jax.random.key(seed)
        ks = jax.random.split(key, 5)

        def w(k, shape, fan_in):
            return jax.random.normal(k, shape, jnp.float32) * fan_in ** (-0.5)
        return {'x': jax.random.normal(ks[0], (B, S, DIN), jnp.float32), 'wq': w(ks[1], (DIM, DIN), DIN), 'wk': w(ks[2], (NKV * HD, DIN), DIN), 'wv': w(ks[3], (NKV * HD, DIN), DIN), 'wo': w(ks[4], (DIM, DIM), DIM)}
    _L0_attn_in = _L0_attn_setup()

    def _L0_ffn_setup():
        import jax, jax.numpy as jnp
        import numpy as np
        B, S, DIM, FFN, E = (4, 256, 128, 512, 8)
        key = jax.random.key(seed)
        k0, k1, k2, k3 = jax.random.split(key, 4)
        scale = 0.02
        return {'hidden_states': jax.random.normal(k0, (B, S, DIM), jnp.float32), 'router_w': jax.random.normal(k1, (DIM, E), jnp.float32) * scale, 'router_b': jnp.zeros((E,), jnp.float32), 'w1': jax.random.normal(k2, (E, DIM, 2 * FFN), jnp.float32) * scale, 'w2': jax.random.normal(k3, (E, FFN, DIM), jnp.float32) * scale}
    _L0_ffn_in = _L0_ffn_setup()

    def _L1_attn_setup():
        import jax, jax.numpy as jnp
        import numpy as np
        D_MODEL = 128
        N_HEADS = 16
        HEAD_DIM = D_MODEL // N_HEADS
        KV_LATENT = 32
        LN_EPS = 1e-05

        def apply_rope(x):
            b, h, t, d = x.shape
            half = d // 2
            pos = jnp.arange(t, dtype=x.dtype)[:, None]
            inv_freq = 1.0 / 10000.0 ** (jnp.arange(half, dtype=x.dtype) / half)
            angles = pos * inv_freq[None, :]
            sin = jnp.sin(angles)[None, None]
            cos = jnp.cos(angles)[None, None]
            x1, x2 = (x[..., :half], x[..., half:])
            return jnp.concatenate([x1 * cos - x2 * sin, x1 * sin + x2 * cos], axis=-1)
        key = jax.random.key(seed)
        ks = jax.random.split(key, 6)
        d, L = (D_MODEL, KV_LATENT)
        s = 1.0 / np.sqrt(d)
        sl = 1.0 / np.sqrt(L)
        return {'x': jax.random.normal(ks[0], (2, 256, d), dtype=jnp.float32), 'W_q': jax.random.uniform(ks[1], (d, d), jnp.float32, -s, s), 'W_dkv': jax.random.uniform(ks[2], (d, L), jnp.float32, -s, s), 'W_uk': jax.random.uniform(ks[3], (L, d), jnp.float32, -sl, sl), 'W_uv': jax.random.uniform(ks[4], (L, d), jnp.float32, -sl, sl), 'W_o': jax.random.uniform(ks[5], (d, d), jnp.float32, -s, s), 'ln_gamma': jnp.ones((L,), jnp.float32), 'ln_beta': jnp.zeros((L,), jnp.float32)}
    _L1_attn_in = _L1_attn_setup()

    def _L1_ffn_setup():
        import jax, jax.numpy as jnp
        import numpy as np
        D, H, O, E, TOPK = (128, 512, 128, 8, 2)
        B, L = (2, 256)
        ROUTE_SCALE = 1.0
        key = jax.random.key(seed)
        ks = jax.random.split(key, 7)
        gb = float(np.sqrt(6.0 / (E + D)))
        return {'x': jax.random.normal(ks[0], (B, L, D), dtype=jnp.float32), 'gate_w': jax.random.uniform(ks[1], (E, D), jnp.float32, -gb, gb), 'gate_b': jnp.zeros((E,), jnp.float32), 'w1': jax.random.normal(ks[2], (E, D, H), jnp.float32) * 0.02, 'b1': jnp.zeros((E, H), jnp.float32), 'w2': jax.random.normal(ks[3], (E, H, O), jnp.float32) * 0.02, 'b2': jnp.zeros((E, O), jnp.float32)}
    _L1_ffn_in = _L1_ffn_setup()
    _d = {'L0_attn_x': _L0_attn_in['x'], 'L0_attn_wq': _L0_attn_in['wq'], 'L0_attn_wk': _L0_attn_in['wk'], 'L0_attn_wv': _L0_attn_in['wv'], 'L0_attn_wo': _L0_attn_in['wo'], 'L0_ffn_router_w': _L0_ffn_in['router_w'], 'L0_ffn_router_b': _L0_ffn_in['router_b'], 'L0_ffn_w1': _L0_ffn_in['w1'], 'L0_ffn_w2': _L0_ffn_in['w2'], 'L1_attn_W_q': _L1_attn_in['W_q'], 'L1_attn_W_dkv': _L1_attn_in['W_dkv'], 'L1_attn_W_uk': _L1_attn_in['W_uk'], 'L1_attn_W_uv': _L1_attn_in['W_uv'], 'L1_attn_W_o': _L1_attn_in['W_o'], 'L1_attn_ln_gamma': _L1_attn_in['ln_gamma'], 'L1_attn_ln_beta': _L1_attn_in['ln_beta'], 'L1_ffn_gate_w': _L1_ffn_in['gate_w'], 'L1_ffn_gate_b': _L1_ffn_in['gate_b'], 'L1_ffn_w1': _L1_ffn_in['w1'], 'L1_ffn_b1': _L1_ffn_in['b1'], 'L1_ffn_w2': _L1_ffn_in['w2'], 'L1_ffn_b2': _L1_ffn_in['b2']}
    _x0 = _d['L0_attn_x']
    _d['L0_attn_x'] = jax.random.normal(jax.random.fold_in(jax.random.key(seed), 1), (8, 512, 128), dtype=_x0.dtype)
    del _x0
    return _d

def reference(L0_attn_x, L0_attn_wq, L0_attn_wk, L0_attn_wv, L0_attn_wo, L0_ffn_router_w, L0_ffn_router_b, L0_ffn_w1, L0_ffn_w2, L1_attn_W_q, L1_attn_W_dkv, L1_attn_W_uk, L1_attn_W_uv, L1_attn_W_o, L1_attn_ln_gamma, L1_attn_ln_beta, L1_ffn_gate_w, L1_ffn_gate_b, L1_ffn_w1, L1_ffn_b1, L1_ffn_w2, L1_ffn_b2):

    def _L0_attn_ref(x, wq, wk, wv, wo):
        import jax, jax.numpy as jnp
        import numpy as np
        B, S, DIN, DIM = (1, 512, 128, 128)
        NH, NKV = (16, 4)
        HD = DIM // NH
        GS = NH // NKV
        b, s, _ = x.shape
        q = (x @ wq.T).reshape(b, s, NKV, GS, HD)
        k = (x @ wk.T).reshape(b, s, NKV, HD)
        v = (x @ wv.T).reshape(b, s, NKV, HD)
        scale = jnp.asarray(HD ** 0.5, x.dtype)
        att = jnp.einsum('bsgmd,btgd->bgmst', q, k) / scale
        causal = jnp.triu(jnp.ones((s, s), bool), 1)
        att = jnp.where(causal, -jnp.inf, att)
        att = jax.nn.softmax(att, axis=-1)
        ctx = jnp.einsum('bgmst,btgd->bsgmd', att, v).reshape(b, s, DIM)
        return ctx @ wo.T

    def _L0_ffn_ref(hidden_states, router_w, router_b, w1, w2):
        import jax, jax.numpy as jnp
        import numpy as np
        B, S, DIM, FFN, E = (4, 256, 128, 512, 8)
        b, s, d = hidden_states.shape
        x = hidden_states.reshape(-1, d)
        logits = x @ router_w + router_b
        route = jax.nn.softmax(logits, axis=1)
        max_prob = jnp.max(route, axis=1, keepdims=True)
        max_ind = jnp.argmax(route, axis=1)
        out = jnp.zeros_like(x)
        num_experts = w1.shape[0]
        for e in range(num_experts):
            h = x @ w1[e]
            a, g = jnp.split(h, 2, axis=1)
            y = jax.nn.silu(a) * g @ w2[e]
            out = jnp.where((max_ind == e)[:, None], y, out)
        out = out * max_prob
        return out.reshape(b, s, d)

    def _L1_attn_ref(x, W_q, W_dkv, W_uk, W_uv, W_o, ln_gamma, ln_beta):
        import jax, jax.numpy as jnp
        import numpy as np
        D_MODEL = 128
        N_HEADS = 16
        HEAD_DIM = D_MODEL // N_HEADS
        KV_LATENT = 32
        LN_EPS = 1e-05

        def apply_rope(x):
            b, h, t, d = x.shape
            half = d // 2
            pos = jnp.arange(t, dtype=x.dtype)[:, None]
            inv_freq = 1.0 / 10000.0 ** (jnp.arange(half, dtype=x.dtype) / half)
            angles = pos * inv_freq[None, :]
            sin = jnp.sin(angles)[None, None]
            cos = jnp.cos(angles)[None, None]
            x1, x2 = (x[..., :half], x[..., half:])
            return jnp.concatenate([x1 * cos - x2 * sin, x1 * sin + x2 * cos], axis=-1)
        b, t, _ = x.shape
        q = (x @ W_q).reshape(b, t, N_HEADS, HEAD_DIM).transpose(0, 2, 1, 3)
        lat = x @ W_dkv
        mu = jnp.mean(lat, axis=-1, keepdims=True)
        var = jnp.mean(jnp.square(lat - mu), axis=-1, keepdims=True)
        lat = (lat - mu) * jax.lax.rsqrt(var + LN_EPS) * ln_gamma + ln_beta
        k = (lat @ W_uk).reshape(b, t, N_HEADS, HEAD_DIM).transpose(0, 2, 1, 3)
        v = (lat @ W_uv).reshape(b, t, N_HEADS, HEAD_DIM).transpose(0, 2, 1, 3)
        q = apply_rope(q)
        k = apply_rope(k)
        scores = jnp.einsum('bhqd,bhkd->bhqk', q, k) / jnp.sqrt(jnp.float32(HEAD_DIM))
        causal = jnp.tril(jnp.ones((t, t), dtype=bool))
        scores = jnp.where(causal[None, None], scores, -jnp.inf)
        attn = jax.nn.softmax(scores, axis=-1)
        out = jnp.einsum('bhqk,bhkd->bhqd', attn, v)
        out = out.transpose(0, 2, 1, 3).reshape(b, t, D_MODEL)
        return out @ W_o

    def _L1_ffn_ref(x, gate_w, gate_b, w1, b1, w2, b2):
        import jax, jax.numpy as jnp
        import numpy as np
        D, H, O, E, TOPK = (128, 512, 128, 8, 2)
        B, L = (2, 256)
        ROUTE_SCALE = 1.0
        Bb, Ll, Dd = x.shape
        N = Bb * Ll
        x_flat = x.reshape(N, Dd)
        logits = x_flat @ gate_w.T + gate_b
        probs = jax.nn.softmax(logits * ROUTE_SCALE, axis=-1)
        topk_vals, topk_idx = jax.lax.top_k(probs, TOPK)
        dense_gate = jnp.zeros((N, E), probs.dtype).at[jnp.arange(N)[:, None], topk_idx].set(topk_vals)
        h = jax.nn.relu(jnp.einsum('nd,edh->neh', x_flat, w1) + b1)
        y = jnp.einsum('neh,eho->neo', h, w2) + b2
        out_flat = jnp.einsum('ne,neo->no', dense_gate, y)
        return out_flat.reshape(Bb, Ll, O)
    x = L0_attn_x
    x = x + _L0_attn_ref(_layernorm(x, axis=-1), L0_attn_wq, L0_attn_wk, L0_attn_wv, L0_attn_wo)
    x = x + _L0_ffn_ref(_layernorm(x, axis=-1), L0_ffn_router_w, L0_ffn_router_b, L0_ffn_w1, L0_ffn_w2)
    x = x + _L1_attn_ref(_layernorm(x, axis=-1), L1_attn_W_q, L1_attn_W_dkv, L1_attn_W_uk, L1_attn_W_uv, L1_attn_W_o, L1_attn_ln_gamma, L1_attn_ln_beta)
    x = x + _L1_ffn_ref(_layernorm(x, axis=-1), L1_ffn_gate_w, L1_ffn_gate_b, L1_ffn_w1, L1_ffn_b1, L1_ffn_w2, L1_ffn_b2)
    return x

_drawn_inputs = setup_inputs


def setup_inputs(seed=0):
    import zlib

    import numpy as np

    out = dict(_drawn_inputs(seed))
    spreads = {'L0_ffn_router_b': (0.0, 0.8),
     'L1_attn_ln_gamma': (1.0, 0.6),
     'L1_attn_ln_beta': (0.0, 0.747),
     'L1_ffn_gate_b': (0.0, 2.0),
     'L1_ffn_b1': (0.0, 2.0),
     'L1_ffn_b2': (0.0, 0.677)}
    factors = {'L0_ffn_router_w': 8.0,
     'L0_ffn_w1': 8.0,
     'L0_ffn_w2': 8.0,
     'L1_attn_W_q': 3.374,
     'L1_attn_W_uk': 3.405,
     'L1_ffn_gate_w': 2.688,
     'L1_ffn_w1': 7.191,
     'L1_ffn_w2': 2.84}
    for name, (base, spread) in spreads.items():
        noise = np.random.default_rng([zlib.crc32(name.encode()), seed]).standard_normal(out[name].shape)
        drawn = base * np.exp(spread * noise) if base else spread * noise
        out[name] = jnp.asarray(drawn.astype(out[name].dtype))
    for name, factor in factors.items():
        out[name] = (out[name] * factor).astype(out[name].dtype)
    return out
```

```python
import concourse.bass as bass
from concourse import mybir
from contextlib import ExitStack

F32 = mybir.dt.float32
BF16 = mybir.dt.bfloat16
I32 = mybir.dt.int32
ALU = mybir.AluOpType
ACT = mybir.ActivationFunctionType
AX = mybir.AxisListType.X

P = 128
BATCHES, SEQ, DIM = 8, 512, 128
QT = SEQ // P
TILES = BATCHES * QT
HEADS, HD = 16, 8
KV0 = 4
LATENT = 32
EXPERTS = 8
FFN = 512
FCH = FFN // P
HALVES = 2
GB = BATCHES // HALVES
GT = GB * QT
TOPK = (1, 2)
SLOTS = tuple(GT * k + EXPERTS - 1 for k in TOPK)
MAXSLOTS = max(SLOTS)
EPS = 1e-5
SCALE = float(HD) ** -0.5
NEG = -3.0e38
VW = HD + 1
CW = 32
PARTS_OF_Q = (0, 0, 1, 1, 0, 2)
PARTS_OF_K = (0, 1, 0, 1, 2, 0)
MAXROW = 96
UNITS = (((0, 0),), ((1, 0),), ((2, 0), (3, 256)))

C_ID, C_MASK, C_TRI, C_FIRST, C_ONE = 0, 128, 256, 384, 512
C_RANK, C_THR, C_SLOT, C_HALF = 640, 648, 664, 712
C_ALL = 716


class Ticket:

    def __init__(self, queue, at):
        self.queue, self.at, self.used, self.value = queue, at, False, None


class Landed:

    def __init__(self, sem, value):
        self.sem, self.value = sem, value


class Queue:

    def __init__(self, sem):
        self.sem, self.steps, self.seen = sem, [], {}

    def wait(self, *points):
        for p in points:
            if isinstance(p, Landed):
                key, at = id(p.sem), p.value
            else:
                key, at = id(p.queue), p.at
            if self.seen.get(key, -1) < at:
                self.seen[key] = at
                if isinstance(p, Ticket):
                    p.used = True
                self.steps.append(p)

    def do(self, make):
        ticket = Ticket(self, len(self.steps))
        self.steps.append((ticket, make))
        return ticket

    def count(self):
        n = 0
        for s in self.steps:
            if isinstance(s, tuple) and s[0].used:
                n += 1
                s[0].value = n

    def emit(self, eng):
        for s in self.steps:
            if isinstance(s, Landed):
                eng.wait_ge(s.sem, s.value)
            elif isinstance(s, Ticket):
                eng.wait_ge(s.queue.sem, s.value)
            else:
                ins = s[1](eng)
                if s[0].used:
                    ins.then_inc(self.sem, 1)


class Stream:

    def __init__(self, sem):
        self.sem, self.sent = sem, 0

    def start(self, queue, make):
        queue.do(lambda e: make(e).then_inc(self.sem, 16))
        self.sent += 16
        return Landed(self.sem, self.sent)


class Slot:

    def __init__(self, ap):
        self.ap, self.freed, self.taken = ap[:], [], False

    def free(self, *points):
        self.freed, self.taken = list(points), False


class Ring:
    def __init__(self, slots):
        self.slots, self.at = slots, -1

    def next(self):
        self.at += 1
        slot = self.slots[self.at % len(self.slots)]
        assert not slot.taken, "taken again before its readers are in the program"
        slot.taken = True
        return slot


def weave(*streams):
    live = [[g, n, 0] for g, n in streams]
    while live:
        s = min(live, key=lambda x: (x[2] + 0.5) / x[1])
        try:
            next(s[0])
            s[2] += 1
        except StopIteration:
            live.remove(s)


def two_layers(nc, d):
    ctx = ExitStack()
    with ctx:
        def sb(name, shape, dt=F32):
            return ctx.enter_context(nc.sbuf_tensor(name, shape, dt))

        def sem(name):
            return ctx.enter_context(nc.semaphore(name))

        pe, act, dve, pool, sp = (Queue(sem(n)) for n in ("pe_done", "act_done", "dve_done", "pool_done", "sp_done"))

        X = sb("X", [P, TILES, DIM])
        consts = sb("consts", [P, C_ALL])
        ident_bf = sb("ident_bf", [P, P], BF16)
        mask_bf = sb("mask_bf", [P, P], BF16)
        tri_bf = sb("tri_bf", [P, P], BF16)
        ones_bf = sb("ones_bf", [P, P], BF16)
        cos_t = sb("cos_t", [P, SEQ])
        sin_t = sb("sin_t", [P, SEQ])
        wq0, wo0 = sb("wq0", [P, P]), sb("wo0", [P, P])
        wkv0 = sb("wkv0", [P, 2, KV0 * HD])
        wq1, wq1_sw, wo1 = sb("wq1", [P, P]), sb("wq1_sw", [P, P]), sb("wo1", [P, P])
        wdkv = sb("wdkv", [P, LATENT])
        wu1 = sb("wu1", [LATENT, 3, P])
        ln_gb = sb("ln_gb", [P, 2, LATENT])
        router = [sb("router0", [P, EXPERTS]), sb("router1", [P, EXPERTS])]
        router_b = sb("router_b", [P, 2, EXPERTS])
        big = sb("expert_weights", [P, EXPERTS * FFN * 3])
        n1 = EXPERTS * FFN
        w1 = [big[:, 0:2 * n1].rearrange("p (e n) -> p e n", e=EXPERTS),
              big[:, 0:n1].rearrange("p (e n) -> p e n", e=EXPERTS)]
        w2 = [big[:, 2 * n1:3 * n1].rearrange("p (e n) -> p e n", e=EXPERTS),
              big[:, n1:2 * n1].rearrange("p (e n) -> p e n", e=EXPERTS)]
        b1_all = big[:, 2 * n1:3 * n1].rearrange("p (e n) -> p e n", e=EXPERTS)
        b2_all = sb("b2_all", [P, EXPERTS, DIM])

        q_stack = [sb(f"q_stack{i}", [P, HEADS, SEQ], BF16) for i in range(2)]
        k_stack = [sb(f"k_stack{i}", [P, HEADS, SEQ], BF16) for i in range(2)]
        VROW = HEADS * VW + CW - VW
        values = [sb(f"values{i}", [P, QT, VROW]) for i in range(2)]
        scratch = sb("scratch", [P, 3 * 4 * SEQ])
        scr3 = scratch[:, :].rearrange("p (s c n) -> p s c n", s=3, c=4)
        expd = Ring([Slot(scr3[:, i]) for i in range(3)])
        scr12 = scratch[:, :].rearrange("p (s n) -> p s n", s=12)
        rows_in = Ring([Slot(scr12[:, i]) for i in (0, 1)])
        rows_t = Ring([Slot(scr12[:, i]) for i in (2, 3)])
        silu_a = Ring([Slot(scr12[:, i]) for i in (4, 5)])
        hidden = Ring([Slot(scr12[:, i]) for i in (6, 7)])
        hidden_t = Ring([Slot(scr12[:, i]) for i in (8, 9)])
        rows_out = Ring([Slot(scr12[:, i]) for i in (10, 11)])

        xn_half = sb("xn_half", [P, GT, DIM])
        xn_half_slots = [Slot(xn_half[:, QT * i:QT * i + QT]) for i in range(GB)]
        gathered = Ring([Slot(sb(f"gathered{i}", [P, DIM])) for i in range(4)])
        gather_streams = [Stream(sem(f"gathered_sem{i}")) for i in range(4)]
        xn = Slot(sb("xn", [P, QT, DIM]))
        xn_t = Ring([Slot(sb(f"xn_t{i}", [P, SEQ])) for i in range(2)])
        rot = [Slot(sb(f"rot{i}", [P, SEQ])) for i in range(2)]
        exact, rest = rot
        parts = Ring([Slot(sb("parts", [P, 3, SEQ], BF16))])
        lat_n = Slot(sb("lat_n", [P, QT, LATENT]))
        lat_t = Slot(sb("lat_t", [LATENT, SEQ]))
        neg_max = [Slot(sb(f"neg_max{i}", [P, QT * HEADS])) for i in range(2)]
        max_parts = Slot(sb("max_parts", [QT * HEADS, 3, P], BF16))
        max_rest = Slot(sb("max_rest", [QT * HEADS, P]))
        ctx_raw = Slot(sb("ctx_raw", [P, SEQ]))
        ctx_rec = Slot(sb("ctx_rec", [P, QT, 4]))
        ctx_n = Slot(sb("ctx_n", [P, QT, DIM]))
        ln_small = Ring([Slot(sb(f"ln_small{i}", [P, QT, 10])) for i in range(2)])
        logits = Slot(sb("logits", [P, GT, EXPERTS]))
        R = [sb(f"route{i}", [P, GT, EXPERTS]) for i in range(6)]
        r_small = sb("route_small", [P, 4, GT])
        onehot = [sb(f"onehot{k}", [P, GT, EXPERTS]) for k in range(2)]
        chosen = sb("chosen", [P, EXPERTS, GT], BF16)
        e_small = sb("e_small", [P, 4, EXPERTS])
        slot_cmp = sb("slot_cmp", [1, MAXSLOTS, EXPERTS])
        slot_f = sb("slot_f", [1, MAXSLOTS])
        gates = [[sb(f"gate{g}{k}", [P, GT]) for k in range(2)] for g in range(HALVES)]
        rows_of = [[sb(f"rows_of{g}{k}", [P, GT], I32) for k in range(2)] for g in range(HALVES)]
        expert_of = [sb(f"expert_of{g}", [1, MAXSLOTS], I32) for g in range(HALVES)]

        psum = ctx.enter_context(nc.psum_tensor("psum", [P, 8, SEQ], F32))
        bank = [Slot(psum[:, i, :]) for i in range(8)]
        max_banks = Ring(bank[0:3])
        score_banks = Ring(bank[3:5])
        value_bank = bank[5]
        misc = Ring(bank[6:8])

        sorted_in = [nc.dram_tensor(f"sorted_in{g}", (MAXSLOTS * P, DIM), F32, kind="Internal").ap() for g in range(HALVES)]
        sorted_out = [nc.dram_tensor(f"sorted_out{g}", (MAXSLOTS * P, DIM), F32, kind="Internal").ap() for g in range(HALVES)]

        parts_out = {(n, i): nc.dram_tensor(f"{n}_parts{i}", (3, P, SEQ), BF16, kind="Internal").ap() for n in "qk" for i in range(2)}
        max_out = [nc.dram_tensor(f"max_parts_out{i}", (3, QT * HEADS, P), BF16, kind="Internal").ap() for i in range(2)]

        ident = consts[:, C_ID:C_ID + P]

        def mm(out, lhsT, rhs, start=True, stop=True):
            return pe.do(lambda e: e.matmul(out, lhsT, rhs, start=start, stop=stop))

        def transpose(out, in_, idn):
            return pe.do(lambda e: e.transpose(out, in_, idn))

        def func(out, in_, f, scale=1.0):
            return act.do(lambda e: e.activation(out, in_, f, scale=scale))

        def copy_a(out, in_):
            return func(out, in_, ACT.Copy)

        def copy_v(out, in_):
            return dve.do(lambda e: e.tensor_copy(out, in_))

        def tt(out, a, b, op, q=dve):
            return q.do(lambda e: e.tensor_tensor(out, a, b, op))

        def ts(out, a, s1, s2, op0, op1=ALU.bypass):
            return dve.do(lambda e: e.tensor_scalar(out, a, s1, s2, op0, op1))

        def stt(out, a, s, b, op0, op1):
            return dve.do(lambda e: e.scalar_tensor_tensor(out=out, in0=a, scalar=s, in1=b, op0=op0, op1=op1))

        def reduce(out, in_, op, negate=False):
            return dve.do(lambda e: e.tensor_reduce(out=out, in_=in_, axis=AX, op=op, negate=negate))

        def scan(out, keep, add):
            return dve.do(lambda e: e.tensor_tensor_scan(out, keep, add, 0.0, ALU.mult, ALU.add))

        def dma(stream, out, in_, q=sp):
            return stream.start(q, lambda e: e.dma_start(out, in_))

        load_x = [Stream(sem(f"load_x{b}")) for b in range(BATCHES)]
        x_ready = [None] * BATCHES
        x_view = d["x"].rearrange("b (t p) d -> b p t d", p=P)
        load_c = Stream(sem("load_consts"))
        load_a = Stream(sem("load_attention_weights"))
        load_w = Stream(sem("load_expert_weights"))

        def load_batch(b):
            x_ready[b] = dma(load_x[b], X[:, QT * b:QT * b + QT, :], x_view[b])

        load_batch(0)
        got_consts = dma(load_c, consts[:, :], d["consts"])
        for out, in_ in ((wq0[:, :], d["wq0"]), (wkv0[:, 0, :], d["wk0"]), (wkv0[:, 1, :], d["wv0"]), (wo0[:, :], d["wo0"])):
            got_attention = dma(load_a, out, in_)
        load_batch(1)
        got_attention1 = None
        load_a1 = Stream(sem("load_attention1_weights"))
        for out, in_ in ((router[0][:, :], d["router0"]), (router[1][:, :], d["router1"]),
                         (router_b[:, 0, :], d["router_b0"].partition_broadcast(P)),
                         (router_b[:, 1, :], d["router_b1"].partition_broadcast(P)),
                         (wq1[:, :], d["wq1"]), (wq1_sw[:, :], d["wq1_sw"]), (wo1[:, :], d["wo1"]), (wdkv[:, :], d["wdkv"]),
                         (wu1[:, 0, :], d["wuk"]), (wu1[:, 1, :], d["wuk_sw"]), (wu1[:, 2, :], d["wuv"]),
                         (ln_gb[:, 0, :], d["ln_gamma"].partition_broadcast(P)),
                         (ln_gb[:, 1, :], d["ln_beta"].partition_broadcast(P)),
                         (b2_all[:, :, :], d["b2"].rearrange("e n -> (e n)").partition_broadcast(P).rearrange("p (e n) -> p e n", e=EXPERTS)),
                         (cos_t[:, :], d["cos"]), (sin_t[:, :], d["sin"])):
            got_attention1 = dma(load_a1, out, in_)
        for b in range(2, BATCHES):
            load_batch(b)
        got_w0 = []
        for e in range(EXPERTS):
            dma(load_w, w1[0][:, e, :], d["w1_0"][e])
        got_w0 = dma(load_w, w2[0].rearrange("p e (c n) -> p e c n", c=FCH), d["w2_0"].rearrange("e (c p) n -> p e c n", p=P))

        zeroed = dve.do(lambda e: e.memset(xn_half[:, :, :], 0.0))
        stacks_set = []
        for i in range(2):
            stacks_set.append(dve.do(lambda e, i=i: e.memset(q_stack[i][:, :, :].bitcast(F32), 0.0)))
            z = pool.do(lambda e, i=i: e.memset(k_stack[i][:, :, :].bitcast(F32), 0.0))
            pool.wait(z)
            z = pool.do(lambda e, i=i: e.memset(k_stack[i][MAXROW:P, :, :], 1.0))
            stacks_set.append(z)
            pool.wait(z)
            stacks_set.append(pool.do(lambda e, i=i: e.memset(values[i][:, :, :], 1.0)))
        dve.wait(got_consts)
        for out, c in ((ident_bf, C_ID), (mask_bf, C_MASK), (tri_bf, C_TRI), (ones_bf, C_ONE)):
            bf_ready = copy_v(out[:, :], consts[:, c:c + P])
        for q in (pe, act, pool, sp):
            q.wait(got_consts)
        pe.wait(bf_ready, *stacks_set)
        sp.wait(*stacks_set)
        act.wait(*stacks_set)
        zero_fill = Stream(sem("zero_fill"))
        sp.wait(zeroed)
        for g in range(HALVES):
            for s in range(0, MAXSLOTS, GT):
                n = min(GT, MAXSLOTS - s)
                filled = dma(zero_fill, sorted_in[g][s * P:(s + n) * P, :].rearrange("(t p) d -> p t d", p=P), xn_half[:, 0:n, :])
        for s in xn_half_slots:
            s.free(filled)

        def row_stats(width, src):
            s = ln_small.next()
            st, mv, ve, rs = s.ap[:, :, 0:6], s.ap[:, :, 6:8], s.ap[:, :, 8:9], s.ap[:, :, 9:10]
            dve.wait(*s.freed)
            for t in range(QT):
                a = dve.do(lambda e, t=t: e.bn_stats(st[:, t, :], src(t)))
            dve.wait(a)
            for t in range(QT):
                a = dve.do(lambda e, t=t: e.bn_aggr(mv[:, t, :], st[:, t, :]))
            dve.wait(a)
            a = ts(ve, mv[:, :, 1:2], EPS, None, ALU.add)
            pool.wait(a)
            a = tt(rs, ve, consts[:, C_HALF:C_HALF + QT].unsqueeze(2), ALU.pow, pool)
            dve.wait(a)
            return s, mv, rs

        def normalise(b, out):
            dve.wait(x_ready[b])
            s, mv, rs = row_stats(DIM, lambda t: X[:, QT * b + t, :])
            for t in range(QT):
                a = ts(out[:, t, :], X[:, QT * b + t, :], mv[:, t, 0:1], rs[:, t, :], ALU.subtract, ALU.mult)
            s.free(a)
            return a

        def transposed_rows(src, ready):
            bk, dst = misc.next(), xn_t.next()
            pe.wait(ready, *bk.freed)
            for t in range(QT):
                a = transpose(bk.ap[:, t * P:(t + 1) * P], src[:, t, :], ident)
            act.wait(a, *dst.freed)
            c = copy_a(dst.ap, bk.ap)
            bk.free(c)
            return dst, c, a

        def split(src, dst, n, rest_slot, release):
            hi = copy_a(dst[:, 0, 0:n], src)
            dve.wait(hi, *rest_slot.freed)
            r = tt(rest_slot.ap[:, 0:n], src, dst[:, 0, 0:n], ALU.subtract)
            release(r, hi)
            act.wait(r)
            mid = copy_a(dst[:, 1, 0:n], rest_slot.ap[:, 0:n])
            pool.wait(mid)
            lo = tt(dst[:, 2, 0:n], rest_slot.ap[:, 0:n], dst[:, 1, 0:n], ALU.subtract, pool)
            rest_slot.freed = [lo]
            return lo

        stack_streams = {(n, i): Stream(sem(f"{n}_stacked{i}")) for n in "qkm" for i in range(2)}
        stack_free = [[], []]
        values_free = [[], []]
        stacked = [None, None]
        maxima_in = [None, None]
        values_in = [None, None]

        park_streams = {(n, i): Stream(sem(f"{n}_parked{i}")) for n in "qkm" for i in range(2)}

        def stack(which, dst, pr, ready, i):
            out = parts_out[which, i]
            sp.wait(ready)
            parked = dma(park_streams[which, i], out.rearrange("s p n -> p s n"), pr.ap)
            pr.free(parked)
            sp.wait(parked, *stack_free[i])
            for r, part in enumerate(PARTS_OF_Q if which == "q" else PARTS_OF_K):
                got = dma(stack_streams[which, i], dst[HD * r:HD * r + HD, :, :],
                          out[part].rearrange("(h d) n -> d h n", d=HD))
            return got

        def front0(b):
            i = b % 2
            dve.wait(*xn.freed)
            a = normalise(b, xn.ap)
            yield
            xt, c, a = transposed_rows(xn.ap, a)
            xn.freed = [a]
            yield
            yield
            bk = misc.next()
            pe.wait(got_attention, c, *bk.freed)
            a = mm(bk.ap, wq0[:, :], xt.ap)
            act.wait(a)
            pr = parts.next()
            act.wait(*pr.freed)
            lo = split(bk.ap, pr.ap, SEQ, rest, bk.free)
            gq = stack("q", q_stack[i], pr, lo, i)
            yield
            bk = misc.next()
            pe.wait(*bk.freed)
            for t in range(QT):
                mm(bk.ap[32 * t:32 * t + 32, 0:P], wkv0[:, 0, :], xt.ap[:, t * P:(t + 1) * P])
            for t in range(QT):
                a = mm(bk.ap[:, P + 32 * t:P + 32 * t + 32], xt.ap[:, t * P:(t + 1) * P], wkv0[:, 1, :])
            xt.free(a)
            act.wait(a, *values_free[i])
            v = copy_a(values[i][:, :, 0:KV0 * VW].rearrange("p t (g w) -> p t g w", w=VW)[:, :, :, 0:HD],
                       bk.ap[:, P:2 * P].rearrange("p (t g d) -> p t g d", t=QT, g=KV0))
            values_in[i] = v
            pr = parts.next()
            act.wait(*pr.freed)
            lo = split(bk.ap[:, 0:P], pr.ap, P, rest, bk.free)
            bk.free(*bk.freed, v)
            out = parts_out["k", i][:, :, 0:P]
            sp.wait(lo)
            parked = dma(park_streams["k", i], out.rearrange("s p n -> p s n"), pr.ap[:, :, 0:P])
            pr.free(parked)
            sp.wait(parked, *stack_free[i])
            for r, part in enumerate(PARTS_OF_K):
                for t in range(QT):
                    gk = dma(stack_streams["k", i], k_stack[i][HD * r:HD * r + HD, 0:KV0, t * P:(t + 1) * P],
                             out[part, 32 * t:32 * t + 32].rearrange("(g d) n -> d g n", d=HD))
            stacked[i] = (gq, gk)
            yield

        def rotate(bk0, bk1, ready):
            dve.wait(*ready, *rot[0].freed, *rot[1].freed)
            a = tt(rot[0].ap, bk0.ap, cos_t[:, :], ALU.mult)
            b = tt(rot[1].ap, bk1.ap, sin_t[:, :], ALU.mult)
            bk0.free(a)
            bk1.free(b)
            pool.wait(a, b)
            c = tt(exact.ap, rot[0].ap, rot[1].ap, ALU.add, pool)
            rot[1].freed = [c]
            return c

        def front1(b):
            i = b % 2
            dve.wait(*xn.freed)
            a = normalise(b, xn.ap)
            yield
            xt, c, a = transposed_rows(xn.ap, a)
            xn.freed = [a]
            yield
            bk = misc.next()
            pe.wait(got_attention1, c, *bk.freed)
            for t in range(QT):
                a = mm(bk.ap[:, t * LATENT:(t + 1) * LATENT], xt.ap[:, t * P:(t + 1) * P], wdkv[:, :])
            dve.wait(a)
            s, mv, rs = row_stats(LATENT, lambda t: bk.ap[:, t * LATENT:(t + 1) * LATENT])
            dve.wait(*lat_n.freed)
            for t in range(QT):
                a = ts(lat_n.ap[:, t, :], bk.ap[:, t * LATENT:(t + 1) * LATENT], mv[:, t, 0:1], rs[:, t, :], ALU.subtract, ALU.mult)
            s.free(a)
            bk.free(a)
            dve.wait(a, got_attention1)
            a = tt(lat_n.ap, lat_n.ap, ln_gb[:, 0:1, :].to_broadcast([P, QT, LATENT]), ALU.mult)
            dve.wait(a)
            lat_ready = tt(lat_n.ap, lat_n.ap, ln_gb[:, 1:2, :].to_broadcast([P, QT, LATENT]), ALU.add)
            yield
            bk0, bk1 = misc.next(), misc.next()
            pe.wait(*bk0.freed, *bk1.freed)
            mm(bk0.ap, wq1[:, :], xt.ap)
            a = mm(bk1.ap, wq1_sw[:, :], xt.ap)
            xt.free(a)
            c = rotate(bk0, bk1, [a, got_attention1])
            yield
            pr = parts.next()
            act.wait(c, *pr.freed)
            lo = split(exact.ap, pr.ap, SEQ, rest, exact.free)
            gq = stack("q", q_stack[i], pr, lo, i)
            yield
            bk = misc.next()
            pe.wait(lat_ready, *bk.freed)
            for t in range(QT):
                a = transpose(bk.ap[0:LATENT, t * P:(t + 1) * P], lat_n.ap[:, t, :], ident)
            lat_n.freed = [a]
            act.wait(a, *lat_t.freed)
            c = copy_a(lat_t.ap, bk.ap[0:LATENT, :])
            bk.free(c)
            yield
            yield
            bk0, bk1 = misc.next(), misc.next()
            pe.wait(c, *bk0.freed, *bk1.freed)
            mm(bk0.ap, wu1[:, 0, :], lat_t.ap)
            a = mm(bk1.ap, wu1[:, 1, :], lat_t.ap)
            c = rotate(bk0, bk1, [a])
            yield
            pr = parts.next()
            act.wait(c, *pr.freed)
            lo = split(exact.ap, pr.ap, SEQ, rest, exact.free)
            gk = stack("k", k_stack[i], pr, lo, i)
            yield
            bk = misc.next()
            pe.wait(*bk.freed)
            for t in range(QT):
                a = mm(bk.ap[:, t * P:(t + 1) * P], lat_t.ap[:, t * P:(t + 1) * P], wu1[:, 2, :])
            lat_t.freed = [a]
            act.wait(a, *values_free[i])
            v = copy_a(values[i][:, :, 0:HEADS * VW].rearrange("p t (h w) -> p t h w", w=VW)[:, :, :, 0:HD],
                       bk.ap.rearrange("p (t h d) -> p t h d", t=QT, h=HEADS))
            bk.free(v)
            values_in[i] = v
            stacked[i] = (gq, gk)
            yield

        def kv_of(layer, h):
            return h // (HEADS // KV0) if layer == 0 else h

        def maxima(layer, b):
            i = b % 2
            nm = neg_max[i]
            pe.wait(*stacked[i])
            last = None
            for t in range(QT):
                width = (t + 1) * P
                per = SEQ // width
                for h0 in range(0, HEADS, per):
                    bk = max_banks.next()
                    pe.wait(*bk.freed)
                    for j in range(per):
                        h = h0 + j
                        mm(bk.ap[:, j * width:(j + 1) * width], q_stack[i][0:MAXROW, h, t * P:(t + 1) * P],
                           k_stack[i][0:MAXROW, kv_of(layer, h), 0:width], stop=False)
                        a = mm(bk.ap[:, (j + 1) * width - P:(j + 1) * width], ident_bf[:, :], mask_bf[:, :], start=False)
                    dve.wait(a, *nm.freed)
                    r = reduce(nm.ap[:, t * HEADS + h0:t * HEADS + h0 + per],
                               bk.ap[:, 0:per * width].rearrange("p (j n) -> p j n", j=per), ALU.max, negate=True)
                    bk.free(r)
                    last = r
                    yield
            bk = misc.next()
            pe.wait(last, *bk.freed)
            n = QT * HEADS
            a = transpose(bk.ap[0:n, 0:P], nm.ap, ident)
            nm.freed = [a]
            act.wait(a, *max_parts.freed)
            lo = split(bk.ap[0:n, 0:P], max_parts.ap, P, max_rest, bk.free)
            sp.wait(lo)
            parked = dma(park_streams["m", i], max_out[i].rearrange("s p n -> p s n"), max_parts.ap)
            max_parts.freed = [parked]
            sp.wait(parked, *stack_free[i])
            for t in range(QT):
                got = dma(stack_streams["m", i], q_stack[i][MAXROW:MAXROW + 3, :, t * P:(t + 1) * P],
                          max_out[i][:, t * HEADS:(t + 1) * HEADS, :])
            maxima_in[i] = got
            yield

        def front(layer, b):
            yield from (front0 if layer == 0 else front1)(b)
            yield from maxima(layer, b)

        FRONT_STEPS = (8 + 42, 14 + 42)
        LAG = 2

        def core(layer, b):
            i = b % 2
            wo = wo0 if layer == 0 else wo1
            pe.wait(maxima_in[i], values_in[i])
            waiting = []

            def value_products(quad, u, p, masked):
                pe.wait(masked)
                if u == 0:
                    pe.wait(*value_bank.freed)
                for j, off in UNITS[u]:
                    for c in range(4):
                        col = kv_of(layer, 4 * quad + c) * VW
                        a = mm(value_bank.ap[CW * c:CW * c + CW, j * P:SEQ], values[i][:, j, col:col + CW],
                               p.ap[:, c, off:off + SEQ - j * P], start=(j == 0), stop=(j == QT - 1))
                p.free(a)
                if u == len(UNITS) - 1:
                    act.wait(a, *ctx_raw.freed)
                    cp = copy_a(ctx_raw.ap, value_bank.ap)
                    value_bank.freed = [cp]
                    return cp
                return None

            def normalise_quad(quad, cp):
                bk = misc.next()
                pe.wait(cp, *bk.freed)
                for t in range(QT):
                    a = transpose(bk.ap[:, t * P:(t + 1) * P], ctx_raw.ap[:, t * P:(t + 1) * P], ident)
                ctx_raw.freed = [a]
                v4 = bk.ap.rearrange("p (t c w) -> p t c w", t=QT, c=4)
                dve.wait(a, *ctx_rec.freed)
                r = dve.do(lambda e: e.reciprocal(ctx_rec.ap, v4[:, :, :, HD]))
                dve.wait(r, *ctx_n.freed)
                for t in range(QT):
                    r = tt(ctx_n.ap[:, t, 32 * quad:32 * quad + 32].rearrange("p (c d) -> p c d", c=4), v4[:, t, :, 0:HD],
                           ctx_rec.ap[:, t, :].unsqueeze(2).to_broadcast([P, 4, HD]), ALU.mult)
                ctx_rec.freed = [r]
                bk.free(r)
                return r

            pending = None
            for quad in range(4):
                for u, blocks in enumerate(UNITS):
                    p = expd.next()
                    width = blocks[-1][1] + SEQ - blocks[-1][0] * P
                    for c in range(4):
                        h = 4 * quad + c
                        bk = score_banks.next()
                        pe.wait(*bk.freed)
                        for j, off in blocks:
                            a = mm(bk.ap[:, off:off + SEQ - j * P], k_stack[i][:, kv_of(layer, h), j * P:(j + 1) * P],
                                   q_stack[i][:, h, j * P:SEQ])
                        act.wait(a, *p.freed)
                        x = func(p.ap[:, c, 0:width], bk.ap[:, 0:width], ACT.Exp, SCALE)
                        bk.free(x)
                        yield
                    pool.wait(x)
                    if len(blocks) == 1:
                        diag, pat = p.ap[:, :, 0:P], [[0, 4], [1, P]]
                    else:
                        diag = p.ap.rearrange("p c (s n) -> p c s n", n=256)[:, :, :, 0:P]
                        pat = [[0, 4], [0, 2], [1, P]]
                    masked = pool.do(lambda e, diag=diag, pat=pat: e.affine_select(
                        out=diag, in_=diag, compare_op=ALU.is_ge, fill=0.0, base=0, pattern=pat, channel_multiplier=-1))
                    waiting.append((quad, u, p, masked))
                    if pending:
                        ctx_done = normalise_quad(*pending)
                        pending = None
                    if len(waiting) > LAG:
                        w = waiting.pop(0)
                        cp = value_products(*w)
                        if cp:
                            pending = (w[0], cp)
                    yield
            stack_free[i] = [a]
            while waiting or pending:
                if pending:
                    ctx_done = normalise_quad(*pending)
                    pending = None
                    yield
                if waiting:
                    w = waiting.pop(0)
                    cp = value_products(*w)
                    if cp:
                        pending = (w[0], cp)
                    yield
            values_free[i] = list(expd.slots[expd.at % 3].freed)
            bk = misc.next()
            pe.wait(ctx_done, *bk.freed)
            for t in range(QT):
                a = transpose(bk.ap[:, t * P:(t + 1) * P], ctx_n.ap[:, t, :], ident)
            ctx_n.freed = [a]
            ctx_t = xn_t.next()
            act.wait(a, *ctx_t.freed)
            c = copy_a(ctx_t.ap, bk.ap)
            bk.free(c)
            yield
            yield
            bk = misc.next()
            pe.wait(c, got_attention if layer == 0 else got_attention1, *bk.freed)
            for t in range(QT):
                a = mm(bk.ap[:, t * P:(t + 1) * P], ctx_t.ap[:, t * P:(t + 1) * P], wo[:, :])
            ctx_t.free(a)
            dve.wait(a, x_ready[b])
            rows = X[:, QT * b:QT * b + QT, :]
            r = tt(rows, bk.ap.rearrange("p (t n) -> p t n", t=QT), rows, ALU.add)
            bk.free(r)
            x_ready[b] = r
            yield
            yield from route_rows(layer, b)
            if b % GB == GB - 1:
                yield from route(layer, b // GB)

        CORE_STEPS = 60 + 8 + 8

        logits_in = []

        def route_rows(layer, b):
            g4 = b % GB
            dst = xn_half_slots[g4]
            dve.wait(*dst.freed)
            a = normalise(b, dst.ap)
            xn_ready[g4] = a
            yield
            xt, c, _ = transposed_rows(dst.ap, a)
            yield
            yield
            bk = misc.next()
            pe.wait(c, got_attention1, *bk.freed)
            for t in range(QT):
                a = mm(bk.ap[:, t * EXPERTS:(t + 1) * EXPERTS], xt.ap[:, t * P:(t + 1) * P], router[layer][:, :])
            xt.free(a)
            dve.wait(a, got_attention1, *logits.freed)
            r = tt(logits.ap[:, QT * g4:QT * g4 + QT, :], bk.ap[:, 0:QT * EXPERTS].rearrange("p (t e) -> p t e", t=QT),
                   router_b[:, layer:layer + 1, :].to_broadcast([P, QT, EXPERTS]), ALU.add)
            bk.free(r)
            logits_in.append(r)
            yield

        xn_ready = [None] * GB
        route_free = []
        sent = [None, None]
        tiles_read = [[], []]
        experts_ready = [None, None]
        gates_ready = [None, None]
        scatter_streams = [Stream(sem(f"scattered{g}")) for g in range(HALVES)]

        def route(layer, g):
            shape = [P, GT, EXPERTS]

            def wide(ap):
                return ap.unsqueeze(2).to_broadcast(shape)

            def chain(ticket):
                dve.wait(ticket)
                return ticket

            m, total, ksum, vm = (r_small[:, i, :] for i in range(4))
            dve.wait(logits_in[-1], *route_free)
            chain(reduce(m, logits.ap, ALU.max))
            a = tt(R[0][:, :, :], logits.ap, wide(m), ALU.subtract)
            logits.freed = [a]
            act.wait(a)
            a = func(R[1][:, :, :], R[0][:, :, :], ACT.Exp)
            chain(a)
            chain(reduce(total, R[1][:, :, :], ALU.add))
            chain(dve.do(lambda e: e.reciprocal(total, total)))
            cur = R[1]
            for k in range(TOPK[layer]):
                chain(reduce(m, cur[:, :, :], ALU.max))
                tt(gates[g][k][:, :], m, total, ALU.mult)
                chain(tt(R[2][:, :, :], cur[:, :, :], wide(m), ALU.is_ge))
                chain(tt(R[3][:, :, :], R[2][:, :, :], consts[:, C_RANK:C_RANK + EXPERTS].unsqueeze(1).to_broadcast(shape), ALU.mult))
                chain(reduce(vm, R[3][:, :, :], ALU.max))
                last = chain(tt(onehot[k][:, :, :], R[3][:, :, :], wide(vm), ALU.is_equal))
                if k + 1 < TOPK[layer]:
                    chain(stt(R[4][:, :, :], onehot[k][:, :, :], -2.0, cur[:, :, :], ALU.mult, ALU.add))
                    cur = R[4]
            gates_ready[g] = last
            by_expert = chosen[:, :, :].rearrange("p e t -> p t e")
            if TOPK[layer] == 1:
                a = copy_v(by_expert, onehot[0][:, :, :])
            else:
                a = tt(by_expert, onehot[0][:, :, :], onehot[1][:, :, :], ALU.add)
            yield
            flat = chosen[:, :, :].rearrange("p e t -> p (e t)")
            bk = misc.next()
            pe.wait(a, *bk.freed)
            n = EXPERTS * GT
            mm(bk.ap[:, 0:n], tri_bf[:, :], flat)
            a = mm(bk.ap[:, n:2 * n], ones_bf[:, :], flat)
            dve.wait(a)

            def et(ap):
                return ap.rearrange("p (e t) -> p e t", e=EXPERTS)

            r0, r2, r3, r5 = (R[i][:, :, :].rearrange("p t e -> p (t e)") for i in (0, 2, 3, 5))
            counts, tiles, cum, base = (e_small[:, i, :] for i in range(4))
            chain(scan(r0, consts[:, C_FIRST:C_FIRST + n], bk.ap[:, n:2 * n]))
            chain(copy_v(counts, et(r0)[:, :, GT - 1]))
            chain(tt(et(r2), counts.unsqueeze(2).to_broadcast([P, EXPERTS, GT]),
                     consts[:, C_THR:C_THR + GT].unsqueeze(1).to_broadcast([P, EXPERTS, GT]), ALU.is_gt))
            chain(reduce(tiles, et(r2), ALU.add))
            chain(scan(cum, consts[:, C_ONE:C_ONE + EXPERTS], tiles))
            chain(tt(base, cum, tiles, ALU.subtract))
            chain(tt(r3, r0, bk.ap[:, n:2 * n], ALU.subtract))
            chain(tt(r5, r3, bk.ap[:, 0:n], ALU.add))
            a = chain(stt(et(r3), base.unsqueeze(2).to_broadcast([P, EXPERTS, GT]), float(P), et(r5), ALU.mult, ALU.add))
            bk.free(a)
            places = et(r3).rearrange("p e t -> p t e")
            for k in range(TOPK[layer]):
                chain(tt(R[2][:, :, :], onehot[k][:, :, :], places, ALU.mult))
                chain(reduce(vm, R[2][:, :, :], ALU.add))
                placed = chain(copy_v(rows_of[g][k][:, :], vm))
            ns = SLOTS[layer]
            sc = slot_cmp[:, 0:ns, :]
            chain(tt(sc, consts[0:1, C_SLOT:C_SLOT + ns].unsqueeze(2).to_broadcast([1, ns, EXPERTS]),
                     cum[0:1, :].unsqueeze(1).to_broadcast([1, ns, EXPERTS]), ALU.is_ge))
            chain(reduce(slot_f[:, 0:ns], sc, ALU.add))
            chain(ts(slot_f[:, 0:ns], slot_f[:, 0:ns], float(EXPERTS - 1), None, ALU.min))
            experts_ready[g] = chain(copy_v(expert_of[g][:, 0:ns], slot_f[:, 0:ns]))
            yield
            pool.wait(placed, filled, *xn_ready, *tiles_read[g])
            for t in range(GT):
                for k in range(TOPK[layer]):
                    sent[g] = scatter_streams[g].start(pool, lambda e, t=t, k=k: e.indirect_dma_start(
                        sorted_in[g][:, :], bass.IndirectOffsetOnAxis(ap=rows_of[g][k][:, t:t + 1], axis=0),
                        xn_half[:, t, :], None))
                if t % QT == QT - 1:
                    yield
            for s in xn_half_slots:
                s.free(sent[g])

        def load_layer1_experts():
            sp.wait(*weights_free)
            for e in range(EXPERTS):
                dma(load_w, w1[1][:, e, :], d["w1_1"][e])
            dma(load_w, w2[1].rearrange("p e (c n) -> p e c n", c=FCH), d["w2_1"].rearrange("e (c p) n -> p e c n", p=P))
            return dma(load_w, b1_all, d["b1"].rearrange("e n -> (e n)").partition_broadcast(P).rearrange("p (e n) -> p e n", e=EXPERTS))

        weights_free = []
        in_streams = [Stream(sem(f"rows_in{i}")) for i in range(2)]
        out_streams = [Stream(sem(f"rows_out{i}")) for i in range(2)]
        stored = [[], []]
        gathers_done = [[], []]

        def experts(layer, g, got_w):
            ns = SLOTS[layer]
            hb = Ring(bank[0:4])
            tb = Ring([bank[5], bank[6]])
            side = (bank[4], bank[7])
            pe.wait(got_w, experts_ready[g])
            dve.wait(got_w)
            tiles_read[g] = []
            group = {}

            def fetch(q):
                n = min(4, ns - 4 * q)
                src = rows_in.next()
                sp.wait(sent[g], *src.freed)
                got = dma(in_streams[rows_in.at % 2], src.ap[:, 0:n * P].rearrange("p (t n) -> p t n", t=n),
                          sorted_in[g][4 * q * P:(4 * q + n) * P, :].rearrange("(t p) d -> p t d", p=P))
                tiles_read[g] = [got] + tiles_read[g][:1]
                return src, got, n

            def turn(q, src, got, n):
                bk, dst = side[q % 2], rows_t.next()
                pe.wait(got, *bk.freed)
                for t in range(n):
                    a = transpose(bk.ap[:, t * P:(t + 1) * P], src.ap[:, t * P:(t + 1) * P], ident)
                src.free(a)
                act.wait(a, *dst.freed)
                c = copy_a(dst.ap[:, 0:n * P], bk.ap[:, 0:n * P])
                bk.free(c)
                group[q] = [dst, c, rows_out.next(), n, rows_out.at % 2]

            def first(j):
                dst, c = group[j // 4][0:2]
                h = [hb.next() for _ in range(2 - layer)]
                for x in h:
                    pe.wait(*x.freed)
                pe.wait(c)
                reg = {}

                def load(e):
                    reg["e"] = e.value_load(expert_of[g][0:1, j:j + 1], min_val=0, max_val=EXPERTS - 1)

                pe.steps.append((Ticket(pe, len(pe.steps)), load))
                xs = dst.ap[:, (j % 4) * P:(j % 4 + 1) * P]
                for n, x in enumerate(h):
                    a = pe.do(lambda e, n=n, x=x: e.matmul(
                        x.ap, xs, w1[layer][:, bass.ds(reg["e"], 1), n * FFN:(n + 1) * FFN].rearrange("p a n -> p (a n)"),
                        start=True, stop=True))
                dst.free(a)
                hd = hidden.next()
                if layer == 0:
                    s = silu_a.next()
                    act.wait(a, *s.freed)
                    f = func(s.ap, h[0].ap, ACT.Silu)
                    dve.wait(f, *hd.freed)
                    m = tt(hd.ap, h[1].ap, s.ap, ALU.mult)
                    s.free(m)
                    h[0].free(f)
                    h[1].free(m)
                    return reg, hd, m
                dreg = {}

                def dload(e):
                    dreg["e"] = e.value_load(expert_of[g][0:1, j:j + 1], min_val=0, max_val=EXPERTS - 1)

                dve.wait(experts_ready[g])
                dve.steps.append((Ticket(dve, len(dve.steps)), dload))
                dve.wait(a, *hd.freed)
                m = dve.do(lambda e: e.tensor_tensor(hd.ap, h[0].ap, b1_all[:, bass.ds(dreg["e"], 1), :].rearrange("p a n -> p (a n)"), ALU.add))
                h[0].free(m)
                return reg, hd, m, dreg

            def turn_hidden(j, hd, m):
                bk, ht = tb.next(), hidden_t.next()
                pe.wait(m, *bk.freed)
                for c in range(FCH):
                    a = transpose(bk.ap[:, c * P:(c + 1) * P], hd.ap[:, c * P:(c + 1) * P], ident)
                hd.free(a)
                act.wait(a, *ht.freed)
                c = func(ht.ap, bk.ap, ACT.Copy if layer == 0 else ACT.Relu)
                bk.free(c)
                return ht, c

            def second(j, ht, c, reg, dreg):
                q = j // 4
                out, n, slot = group[q][2:5]
                bk = side[q % 2]
                pe.wait(c)
                if j % 4 == 0:
                    pe.wait(*bk.freed)
                cols = slice((j % 4) * P, (j % 4 + 1) * P)
                for k in range(FCH):
                    a = pe.do(lambda e, k=k: e.matmul(
                        bk.ap[:, cols], ht.ap[:, k * P:(k + 1) * P],
                        w2[layer][:, bass.ds(reg["e"], 1), k * DIM:(k + 1) * DIM].rearrange("p a n -> p (a n)"),
                        start=(k == 0), stop=(k == FCH - 1)))
                ht.free(a)
                weights_free[:] = [a]
                group[q][5:] = group[q][5:] + [dreg]
                if j % 4 == n - 1:
                    dve.wait(a, *out.freed)
                    if layer == 0:
                        done = copy_v(out.ap[:, 0:n * P], bk.ap[:, 0:n * P])
                    else:
                        for x, rg in enumerate(group[q][5:]):
                            done = dve.do(lambda e, x=x, rg=rg: e.tensor_tensor(
                                out.ap[:, x * P:(x + 1) * P], bk.ap[:, x * P:(x + 1) * P],
                                b2_all[:, bass.ds(rg["e"], 1), :].rearrange("p a n -> p (a n)"), ALU.add))
                if j % 4 == n - 1:
                    bk.free(done)
                    sp.wait(done, *gathers_done[g])
                    got = dma(out_streams[slot], sorted_out[g][4 * q * P:(4 * q + n) * P, :].rearrange("(t p) d -> p t d", p=P),
                              out.ap[:, 0:n * P].rearrange("p (t n) -> p t n", t=n))
                    out.free(got)
                    stored[g] = [got] + stored[g][:1]

            stored[g] = []
            quads = (ns + 3) // 4
            fetched = {0: fetch(0)}
            f, t = {}, {}
            for j in range(ns + 2):
                if j < ns:
                    if j % 4 == 0:
                        turn(j // 4, *fetched[j // 4])
                        if j // 4 + 1 < quads:
                            fetched[j // 4 + 1] = fetch(j // 4 + 1)
                    f[j] = first(j)
                if 1 <= j <= ns:
                    t[j - 1] = turn_hidden(j - 1, f[j - 1][1], f[j - 1][2])
                if j >= 2:
                    fj = f[j - 2]
                    second(j - 2, *t[j - 2], fj[0], fj[3] if layer else None)
                yield

        def combine(layer, g):
            pool.wait(*stored[g])
            for t in range(GT):
                b = g * GB + t // QT
                for k in range(TOPK[layer]):
                    s = gathered.next()
                    pool.wait(*s.freed)
                    got = gather_streams[gathered.at % 4].start(pool, lambda e, t=t, k=k, s=s: e.indirect_dma_start(
                        s.ap[:, :], None, sorted_out[g][0:SLOTS[layer] * P, :], bass.IndirectOffsetOnAxis(ap=rows_of[g][k][:, t:t + 1], axis=0)))
                    dve.wait(got, gates_ready[g], x_ready[b])
                    row = X[:, g * GT + t, :]
                    r = stt(row, s.ap[:, :], gates[g][k][:, t:t + 1], row, ALU.mult, ALU.add)
                    s.free(r)
                    x_ready[b] = r
                if layer == 1 and t % QT == QT - 1:
                    sp.wait(x_ready[b])
                    dma(out_stream, d["out"].rearrange("b (t p) d -> b p t d", p=P)[b], X[:, QT * b:QT * b + QT, :])
                yield
            gathers_done[g] = [x_ready[b]]

        out_stream = Stream(sem("out_stored"))

        def run(gen):
            for _ in gen:
                pass

        got_w = got_w0
        for layer in range(2):
            run(front(layer, 0))
            for b in range(BATCHES):
                if b + 1 < BATCHES:
                    weave((core(layer, b), CORE_STEPS), (front(layer, b + 1), int(FRONT_STEPS[layer] * 1.15)))
                else:
                    run(core(layer, b))
            shared = []
            for s in expd.slots:
                shared += s.freed
            rings = (rows_in, rows_t, silu_a, hidden, hidden_t, rows_out)
            for r in rings:
                for s in r.slots:
                    s.freed = list(shared)
            run(experts(layer, 0, got_w))
            weave((experts(layer, 1, got_w), SLOTS[layer] + 2), (combine(layer, 0), GT))
            run(combine(layer, 1))
            route_free[:] = x_ready[:]
            if layer == 0:
                got_w = load_layer1_experts()
                shared = []
                for r in rings:
                    for s in r.slots:
                        shared += s.freed
                for s in expd.slots:
                    s.freed = list(shared)
        sp.wait(Landed(out_stream.sem, out_stream.sent))
        for s in out_streams + scatter_streams:
            sp.wait(Landed(s.sem, s.sent))

        for q in (pe, act, dve, pool, sp):
            q.count()

        block = ctx.enter_context(nc.Block())

        @block.sync
        def _(eng):
            sp.emit(eng)

        @block.scalar
        def _(eng):
            act.emit(eng)

        @block.vector
        def _(eng):
            dve.emit(eng)

        @block.gpsimd
        def _(eng):
            pool.emit(eng)

        @block.tensor
        def _(eng):
            pe.emit(eng)


def constants():
    import numpy as np
    c = np.zeros((P, C_ALL), np.float32)
    p = np.arange(P)
    c[:, C_ID:C_ID + P] = np.eye(P)
    c[:, C_MASK:C_MASK + P] = np.where(p[None, :] > p[:, None], NEG, 0.0)
    c[:, C_TRI:C_TRI + P] = p[:, None] < p[None, :]
    c[:, C_FIRST:C_FIRST + P] = p[None, :] % GT != 0
    c[:, C_ONE:C_ONE + P] = 1.0
    c[:, C_RANK:C_RANK + EXPERTS] = EXPERTS - np.arange(EXPERTS)
    c[:, C_THR:C_THR + GT] = P * np.arange(GT)
    c[:, C_SLOT:C_SLOT + MAXSLOTS] = np.arange(MAXSLOTS)
    c[:, C_HALF:C_HALF + QT] = -0.5
    half = HD // 2
    pos = np.arange(SEQ, dtype=np.float32)[:, None]
    inv = (1.0 / 10000.0 ** (np.arange(half, dtype=np.float32) / half)).astype(np.float32)
    ang = (pos * inv[None, :]).astype(np.float32)
    sin, cos = np.sin(ang).T, np.cos(ang).T
    cos_t = np.tile(np.concatenate([cos, cos], 0), (HEADS, 1))
    sin_t = np.tile(np.concatenate([-sin, sin], 0), (HEADS, 1))
    return c, np.ascontiguousarray(cos_t, np.float32), np.ascontiguousarray(sin_t, np.float32)


def kernel(**inputs):
    import numpy as np
    import concourse.bacc as bacc
    from concourse.bass_utils import run_bass_kernel_spmd as launch

    a = {k: np.asarray(v) for k, v in inputs.items()}
    swap = [h * HD + (x + HD // 2) % HD for h in range(HEADS) for x in range(HD)]
    c, cos_t, sin_t = constants()
    arrays = {
        "x": a["L0_attn_x"], "consts": c, "cos": cos_t, "sin": sin_t,
        "wq0": a["L0_attn_wq"].T, "wk0": a["L0_attn_wk"].T, "wv0": a["L0_attn_wv"].T, "wo0": a["L0_attn_wo"].T,
        "router0": a["L0_ffn_router_w"], "router_b0": a["L0_ffn_router_b"], "w1_0": a["L0_ffn_w1"], "w2_0": a["L0_ffn_w2"],
        "wq1": a["L1_attn_W_q"], "wq1_sw": a["L1_attn_W_q"][:, swap], "wo1": a["L1_attn_W_o"], "wdkv": a["L1_attn_W_dkv"],
        "wuk": a["L1_attn_W_uk"], "wuk_sw": a["L1_attn_W_uk"][:, swap], "wuv": a["L1_attn_W_uv"],
        "ln_gamma": a["L1_attn_ln_gamma"], "ln_beta": a["L1_attn_ln_beta"],
        "router1": a["L1_ffn_gate_w"].T, "router_b1": a["L1_ffn_gate_b"],
        "w1_1": a["L1_ffn_w1"], "b1": a["L1_ffn_b1"], "w2_1": a["L1_ffn_w2"], "b2": a["L1_ffn_b2"],
    }
    arrays = {k: np.ascontiguousarray(v) for k, v in arrays.items()}
    nc = bacc.Bacc("TRN2", target_bir_lowering=False, num_devices=1, dynamic_dma_scratch_size=8192)
    d = {k: nc.dram_tensor(f"in_{k}", v.shape, mybir.dt.from_np(v.dtype), kind="ExternalInput").ap() for k, v in arrays.items()}
    d["out"] = nc.dram_tensor("out_0", (BATCHES, SEQ, DIM), F32, kind="ExternalOutput").ap()
    two_layers(nc, d)
    r = launch(nc, [{f"in_{k}": v for k, v in arrays.items()}], core_ids=[0])
    return r.results[0]["out_0"]
```

```python
import concourse.bass as bass
from concourse import mybir
from contextlib import ExitStack

F32 = mybir.dt.float32
BF16 = mybir.dt.bfloat16
I32 = mybir.dt.int32
ALU = mybir.AluOpType
ACT = mybir.ActivationFunctionType
AX = mybir.AxisListType.X

P = 128
BATCHES, SEQ, DIM = 8, 512, 128
QT = SEQ // P
TILES = BATCHES * QT
HEADS, HD = 16, 8
KV0 = 4
LATENT = 32
EXPERTS = 8
FFN = 512
FCH = FFN // P
HALVES = 2
GB = BATCHES // HALVES
GT = GB * QT
TOPK = (1, 2)
SLOTS = tuple(GT * k + EXPERTS - 1 for k in TOPK)
MAXSLOTS = max(SLOTS)
EPS = 1e-5
SCALE = float(HD) ** -0.5
NEG = -3.0e38
VW = HD + 1
CW = 32
GROUPS = 6
RUNS_OF_Q = ((0, 3, 0, 0), (3, 2, 1, 0), (5, 1, 2, 0))
RUNS_OF_K = ((0, 3, 0, 1), (3, 2, 0, 1), (5, 1, 0, 0))
MAXROW = 96
UNITS = (((0, 0),), ((1, 0),), ((2, 0), (3, 256)))

C_ID, C_FIRST, C_ONE, C_RANK, C_THR, C_SLOT, C_HALF = 0, 128, 256, 264, 272, 288, 328
C_ALL = 332


class Ticket:

    def __init__(self, queue, at):
        self.queue, self.at, self.used, self.value = queue, at, False, None


class Landed:

    def __init__(self, sem, value):
        self.sem, self.value = sem, value


class Queue:

    def __init__(self, sem):
        self.sem, self.steps, self.seen = sem, [], {}

    def wait(self, *points):
        for p in points:
            if isinstance(p, Landed):
                key, at = id(p.sem), p.value
            else:
                key, at = id(p.queue), p.at
            if self.seen.get(key, -1) < at:
                self.seen[key] = at
                if isinstance(p, Ticket):
                    p.used = True
                self.steps.append(p)

    def do(self, make):
        ticket = Ticket(self, len(self.steps))
        self.steps.append((ticket, make))
        return ticket

    def count(self):
        n = 0
        for s in self.steps:
            if isinstance(s, tuple) and s[0].used:
                n += 1
                s[0].value = n

    def emit(self, eng):
        for s in self.steps:
            if isinstance(s, Landed):
                eng.wait_ge(s.sem, s.value)
            elif isinstance(s, Ticket):
                eng.wait_ge(s.queue.sem, s.value)
            else:
                ins = s[1](eng)
                if s[0].used:
                    ins.then_inc(self.sem, 1)


class Stream:

    def __init__(self, sem):
        self.sem, self.sent = sem, 0

    def start(self, queue, make):
        queue.do(lambda e: make(e).then_inc(self.sem, 16))
        self.sent += 16
        return Landed(self.sem, self.sent)


class Slot:

    def __init__(self, ap):
        self.ap, self.freed, self.taken = ap[:], [], False

    def free(self, *points):
        self.freed, self.taken = list(points), False


class Ring:
    def __init__(self, slots):
        self.slots, self.at = slots, -1

    def next(self):
        self.at += 1
        slot = self.slots[self.at % len(self.slots)]
        assert not slot.taken, "taken again before its readers are in the program"
        slot.taken = True
        return slot


def weave(main, steps, *sides):
    live = [[g, n, a, z, 0] for g, n, a, z in sides]

    def advance(s, upto):
        while s[4] < upto:
            s[4] += 1
            try:
                next(s[0])
            except StopIteration:
                live.remove(s)
                return

    at = 0
    for _ in main:
        at += 1
        for s in list(live):
            if at / steps > s[2]:
                advance(s, s[1] * (at / steps - s[2]) / (s[3] - s[2]))
    for s in list(live):
        advance(s, float("inf"))


def two_layers(nc, d):
    ctx = ExitStack()
    with ctx:
        def sb(name, shape, dt=F32):
            return ctx.enter_context(nc.sbuf_tensor(name, shape, dt))

        def sem(name):
            return ctx.enter_context(nc.semaphore(name))

        pe, act, dve, pool, sp = (Queue(sem(n)) for n in ("pe_done", "act_done", "dve_done", "pool_done", "sp_done"))

        X = sb("X", [P, TILES, DIM])
        consts = sb("consts", [P, C_ALL])
        ident_bf = sb("ident_bf", [P, P], BF16)
        mask_bf = sb("mask_bf", [P, P], BF16)
        tri_bf = sb("tri_bf", [P, P], BF16)
        ones_bf = sb("ones_bf", [P, P], BF16)
        cos_t = sb("cos_t", [P, SEQ])
        sin_t = sb("sin_t", [P, SEQ])
        wq0, wo0 = sb("wq0", [P, P]), sb("wo0", [P, P])
        wkv0 = sb("wkv0", [P, 2, KV0 * HD])
        wq1, wq1_sw, wo1 = sb("wq1", [P, P]), sb("wq1_sw", [P, P]), sb("wo1", [P, P])
        wdkv = sb("wdkv", [P, LATENT])
        wu1 = sb("wu1", [LATENT, 3, P])
        ln_gb = sb("ln_gb", [P, 2, LATENT])
        router = [sb("router0", [P, EXPERTS]), sb("router1", [P, EXPERTS])]
        router_b = sb("router_b", [P, 2, EXPERTS])
        big = sb("expert_weights", [P, EXPERTS * FFN * 3])
        n1 = EXPERTS * FFN
        w1 = [big[:, 0:2 * n1].rearrange("p (e n) -> p e n", e=EXPERTS),
              big[:, 0:n1].rearrange("p (e n) -> p e n", e=EXPERTS)]
        w2 = [big[:, 2 * n1:3 * n1].rearrange("p (e n) -> p e n", e=EXPERTS),
              big[:, n1:2 * n1].rearrange("p (e n) -> p e n", e=EXPERTS)]
        b1_all = big[:, 2 * n1:3 * n1].rearrange("p (e n) -> p e n", e=EXPERTS)
        b2_all = sb("b2_all", [P, EXPERTS, DIM])

        q_stack = [sb(f"q_stack{i}", [P, HEADS, SEQ], BF16) for i in range(2)]
        k_stack = [sb(f"k_stack{i}", [P, HEADS, SEQ], BF16) for i in range(2)]
        VROW = HEADS * VW + CW - VW
        values = [sb(f"values{i}", [P, QT, VROW]) for i in range(3)]
        scratch = sb("scratch", [P, 3 * 4 * SEQ])
        scr3 = scratch[:, :].rearrange("p (s c n) -> p s c n", s=3, c=4)
        expd = Ring([Slot(scr3[:, i]) for i in range(3)])
        scr12 = scratch[:, :].rearrange("p (s n) -> p s n", s=12)
        rows_in = Ring([Slot(scr12[:, i]) for i in (0, 1)])
        rows_t = Ring([Slot(scr12[:, i]) for i in (2, 3)])
        silu_a = Ring([Slot(scr12[:, i]) for i in (4, 5)])
        hidden = Ring([Slot(scr12[:, i]) for i in (6, 7)])
        hidden_t = Ring([Slot(scr12[:, i]) for i in (8, 9)])
        rows_out = Ring([Slot(scr12[:, i]) for i in (10, 11)])

        xn_half = sb("xn_half", [P, GT, DIM])
        xn_half_slots = [Slot(xn_half[:, QT * i:QT * i + QT]) for i in range(GB)]
        gathered = Ring([Slot(sb(f"gathered{i}", [P, DIM])) for i in range(4)])
        gather_streams = [Stream(sem(f"gathered_sem{i}")) for i in range(4)]
        xn = Slot(sb("xn", [P, QT, DIM]))
        xn_t = Ring([Slot(sb(f"xn_t{i}", [P, SEQ])) for i in range(3)])
        rot = [Slot(sb(f"rot{i}", [P, SEQ])) for i in range(2)]
        exact, rest = rot
        parts = Ring([Slot(sb("parts", [P, 3, SEQ], BF16))])
        lat_n = Slot(sb("lat_n", [P, QT, LATENT]))
        lat_t = Slot(sb("lat_t", [LATENT, SEQ]))
        neg_max = [Slot(sb(f"neg_max{i}", [P, QT * HEADS])) for i in range(2)]
        max_parts = Slot(sb("max_parts", [QT * HEADS, 3, P], BF16))
        max_rest = Slot(sb("max_rest", [QT * HEADS, P]))
        ctx_raw = Slot(sb("ctx_raw", [P, SEQ]))
        ctx_rec = Slot(sb("ctx_rec", [P, QT, 4]))
        ctx_n = Slot(sb("ctx_n", [P, QT, DIM]))
        ln_small = Ring([Slot(sb(f"ln_small{i}", [P, QT, 10])) for i in range(2)])
        logits = Slot(sb("logits", [P, GT, EXPERTS]))
        R = [sb(f"route{i}", [P, GT, EXPERTS]) for i in range(6)]
        r_small = sb("route_small", [P, 4, GT])
        onehot = [sb(f"onehot{k}", [P, GT, EXPERTS]) for k in range(2)]
        chosen = sb("chosen", [P, EXPERTS, GT], BF16)
        e_small = sb("e_small", [P, 4, EXPERTS])
        slot_cmp = sb("slot_cmp", [1, MAXSLOTS, EXPERTS], BF16)
        slot_f = sb("slot_f", [1, MAXSLOTS])
        gates = [[sb(f"gate{g}{k}", [P, GT]) for k in range(2)] for g in range(HALVES)]
        rows_of = [[sb(f"rows_of{g}{k}", [P, GT], I32) for k in range(2)] for g in range(HALVES)]
        expert_of = [sb(f"expert_of{g}", [1, MAXSLOTS], I32) for g in range(HALVES)]

        psum = ctx.enter_context(nc.psum_tensor("psum", [P, 8, SEQ], F32))
        bank = [Slot(psum[:, i, :]) for i in range(8)]
        max_banks = Ring(bank[0:3])
        score_banks = Ring([bank[3], bank[6]])
        value_bank = bank[5]
        misc = Ring([bank[4], bank[7]])

        sorted_in = [nc.dram_tensor(f"sorted_in{g}", (MAXSLOTS * P, DIM), F32, kind="Internal").ap() for g in range(HALVES)]
        sorted_out = [nc.dram_tensor(f"sorted_out{g}", (MAXSLOTS * P, DIM), F32, kind="Internal").ap() for g in range(HALVES)]

        parts_out = {(n, i): nc.dram_tensor(f"{n}_parts{i}", (P, GROUPS, SEQ), BF16, kind="Internal").ap() for n in "qk" for i in range(2)}
        max_out = [nc.dram_tensor(f"max_parts_out{i}", (3, QT * HEADS, P), BF16, kind="Internal").ap() for i in range(2)]

        ident = consts[:, C_ID:C_ID + P]

        def mm(out, lhsT, rhs, start=True, stop=True):
            return pe.do(lambda e: e.matmul(out, lhsT, rhs, start=start, stop=stop))

        def transpose(out, in_, idn):
            return pe.do(lambda e: e.transpose(out, in_, idn))

        def func(out, in_, f, scale=1.0):
            return act.do(lambda e: e.activation(out, in_, f, scale=scale))

        def copy_a(out, in_):
            return func(out, in_, ACT.Copy)

        def copy_v(out, in_):
            return dve.do(lambda e: e.tensor_copy(out, in_))

        def tt(out, a, b, op, q=dve):
            return q.do(lambda e: e.tensor_tensor(out, a, b, op))

        def ts(out, a, s1, s2, op0, op1=ALU.bypass):
            return dve.do(lambda e: e.tensor_scalar(out, a, s1, s2, op0, op1))

        def stt(out, a, s, b, op0, op1):
            return dve.do(lambda e: e.scalar_tensor_tensor(out=out, in0=a, scalar=s, in1=b, op0=op0, op1=op1))

        def reduce(out, in_, op, negate=False):
            return dve.do(lambda e: e.tensor_reduce(out=out, in_=in_, axis=AX, op=op, negate=negate))

        def scan(out, keep, add):
            return dve.do(lambda e: e.tensor_tensor_scan(out, keep, add, 0.0, ALU.mult, ALU.add))

        def dma(stream, out, in_, q=sp):
            return stream.start(q, lambda e: e.dma_start(out, in_))

        load_x = [Stream(sem(f"load_x{b}")) for b in range(BATCHES)]
        x_ready = [None] * BATCHES
        x_view = d["x"].rearrange("b (t p) d -> b p t d", p=P)
        load_c = Stream(sem("load_consts"))
        load_a = Stream(sem("load_attention_weights"))
        load_w = Stream(sem("load_expert_weights"))

        def load_batch(b):
            x_ready[b] = dma(load_x[b], X[:, QT * b:QT * b + QT, :], x_view[b])

        load_batch(0)
        dma(load_c, consts[:, :], d["consts"])
        got_consts = dma(load_c, scratch[:, 0:2 * P], d["masks"])
        for out, in_ in ((wq0[:, :], d["wq0"]), (wkv0[:, 0, :], d["wk0"]), (wkv0[:, 1, :], d["wv0"]), (wo0[:, :], d["wo0"])):
            got_attention = dma(load_a, out, in_)
        load_batch(1)
        got_attention1 = None
        load_a1 = Stream(sem("load_attention1_weights"))
        for out, in_ in ((router[0][:, :], d["router0"]), (router[1][:, :], d["router1"]),
                         (router_b[:, 0, :], d["router_b0"].partition_broadcast(P)),
                         (router_b[:, 1, :], d["router_b1"].partition_broadcast(P)),
                         (wq1[:, :], d["wq1"]), (wq1_sw[:, :], d["wq1_sw"]), (wo1[:, :], d["wo1"]), (wdkv[:, :], d["wdkv"]),
                         (wu1[:, 0, :], d["wuk"]), (wu1[:, 1, :], d["wuk_sw"]), (wu1[:, 2, :], d["wuv"]),
                         (ln_gb[:, 0, :], d["ln_gamma"].partition_broadcast(P)),
                         (ln_gb[:, 1, :], d["ln_beta"].partition_broadcast(P)),
                         (b2_all[:, :, :], d["b2"].rearrange("e n -> (e n)").partition_broadcast(P).rearrange("p (e n) -> p e n", e=EXPERTS)),
                         (cos_t[:, :], d["cos"]), (sin_t[:, :], d["sin"])):
            got_attention1 = dma(load_a1, out, in_)
        for b in range(2, BATCHES):
            load_batch(b)

        def load_layer0_experts():
            for e in range(EXPERTS):
                dma(load_w, w1[0][:, e, :], d["w1_0"][e])
            return dma(load_w, w2[0].rearrange("p e (c n) -> p e c n", c=FCH), d["w2_0"].rearrange("e (c p) n -> p e c n", p=P))

        PAIR_OF_ONES = 1.0 + 0x3F80 / 2.0 ** 23
        stacks_set = [[], []]

        def set_stacks(i, q):
            q.do(lambda e: e.memset(q_stack[i][:, :, :].bitcast(F32), 0.0))
            z = q.do(lambda e: e.memset(k_stack[i][:, :, :].bitcast(F32), 0.0))
            q.wait(z)
            stacks_set[i] = [q.do(lambda e: e.memset(k_stack[i][MAXROW:P, :, :].bitcast(F32), PAIR_OF_ONES))]

        for i in range(3):
            values_set = pool.do(lambda e, i=i: e.memset(values[i][:, :, :], 1.0))
        pool.wait(values_set)
        set_stacks(0, pool)
        pool.wait(*stacks_set[0])
        zeroed = pool.do(lambda e: e.memset(xn_half[:, :, :], 0.0))
        dve.wait(got_consts)
        copy_v(ident_bf[:, :], ident)
        copy_v(mask_bf[:, :], scratch[:, 0:P])
        dve.do(lambda e: e.memset(ones_bf[:, :], 1.0))
        bf_ready = copy_v(tri_bf[:, :], scratch[:, P:2 * P])
        for slot in expd.slots:
            slot.freed = [bf_ready]
        for q in (pe, act, pool, sp):
            q.wait(got_consts)
        pe.wait(bf_ready)
        act.wait(values_set)

        def fill_with_zeros():
            zero_fill = Stream(sem("zero_fill"))
            sp.wait(zeroed)
            for g in range(HALVES):
                for s in range(0, MAXSLOTS, GT):
                    n = min(GT, MAXSLOTS - s)
                    filled = dma(zero_fill, sorted_in[g][s * P:(s + n) * P, :].rearrange("(t p) d -> p t d", p=P), xn_half[:, 0:n, :])
            for s in xn_half_slots:
                s.free(filled)
            return filled

        def row_stats(src):
            s = ln_small.next()
            st, mv, ve, rs = s.ap[:, :, 0:6], s.ap[:, :, 6:8], s.ap[:, :, 8:9], s.ap[:, :, 9:10]
            dve.wait(*s.freed)
            for t in range(QT):
                a = dve.do(lambda e, t=t, rows=src(t): e.bn_stats(st[:, t, :], rows))
            dve.wait(a)
            for t in range(QT):
                a = dve.do(lambda e, t=t: e.bn_aggr(mv[:, t, :], st[:, t, :]))
            dve.wait(a)
            a = ts(ve, mv[:, :, 1:2], EPS, None, ALU.add)
            pool.wait(a)
            a = tt(rs, ve, consts[:, C_HALF:C_HALF + QT].unsqueeze(2), ALU.pow, pool)
            yield
            dve.wait(a)
            return s, mv, rs

        def normalise(b, out):
            dve.wait(x_ready[b])
            s, mv, rs = yield from row_stats(lambda t: X[:, QT * b + t, :])
            for t in range(QT):
                a = ts(out[:, t, :], X[:, QT * b + t, :], mv[:, t, 0:1], rs[:, t, :], ALU.subtract, ALU.mult)
            s.free(a)
            return a

        def transposed_rows(src, ready):
            bk, dst = misc.next(), xn_t.next()
            pe.wait(ready, *bk.freed)
            for t in range(QT):
                a = transpose(bk.ap[:, t * P:(t + 1) * P], src[:, t, :], ident)
            act.wait(a, *dst.freed)
            c = copy_a(dst.ap, bk.ap)
            bk.free(c)
            return dst, c, a

        def split(src, dst, n, rest_slot, release):
            hi = copy_a(dst[:, 0, 0:n], src)
            dve.wait(hi, *rest_slot.freed)
            r = tt(rest_slot.ap[:, 0:n], src, dst[:, 0, 0:n], ALU.subtract)
            release(r, hi)
            yield
            act.wait(r)
            mid = copy_a(dst[:, 1, 0:n], rest_slot.ap[:, 0:n])
            yield
            pool.wait(mid)
            lo = tt(dst[:, 2, 0:n], rest_slot.ap[:, 0:n], dst[:, 1, 0:n], ALU.subtract, pool)
            rest_slot.freed = [lo]
            yield
            return lo

        stack_streams = {(n, i, f): Stream(sem(f"{n}_stacked{i}{f}")) for n in "qk" for i in range(2) for f in range(2)}
        stack_streams.update({("m", i): Stream(sem(f"m_stacked{i}")) for i in range(2)})
        stack_free = [[], []]
        values_free = [[], [], []]
        stacked = {}
        maxima_in = [None, None]
        values_in = [None, None, None]

        park_streams = {(n, i): Stream(sem(f"{n}_parked{i}")) for n in "qkm" for i in range(2)}

        def park(which, pr, ready, i, n=SEQ):
            out = parts_out[which, i]
            sp.wait(ready)
            for row, rows, part, step in (RUNS_OF_Q if which == "q" else RUNS_OF_K):
                def run_of(ap):
                    return ap[:, part:part + rows, :] if step else ap[:, part:part + 1, :].to_broadcast([ap.shape[0], rows, n])
                if n == SEQ:
                    parked[which, i] = dma(park_streams[which, i], out[:, row:row + rows, :], run_of(pr.ap))
                    continue
                for t in range(QT):
                    parked[which, i] = dma(park_streams[which, i], out[0:KV0 * HD, row:row + rows, t * P:(t + 1) * P],
                                           run_of(pr.ap[32 * t:32 * t + 32, :, 0:n]))
            pr.free(parked[which, i])

        parked = {}

        def load_stacks(layer, b):
            i = b % 2
            for f in range(2):
                for which, dst in (("k", k_stack[i]), ("q", q_stack[i])):
                    heads = (KV0 if layer == 0 and which == "k" else HEADS) // 2
                    sp.wait(parked[which, i], *stacks_set[i], *stack_free[i])
                    stacked[which, i, f] = dma(
                        stack_streams[which, i, f], dst[0:GROUPS * HD, f * heads:(f + 1) * heads, :],
                        parts_out[which, i][f * heads * HD:(f + 1) * heads * HD].rearrange("(h d) r n -> (d r) h n", d=HD))
            parked.pop(("q", i))
            parked.pop(("k", i))

        def front0(b):
            i = b % 2
            dve.wait(*xn.freed)
            a = yield from normalise(b, xn.ap)
            yield
            xt, c, a = transposed_rows(xn.ap, a)
            xn.freed = [a]
            yield
            yield
            bk = misc.next()
            pe.wait(got_attention, c, *bk.freed)
            a = mm(bk.ap, wq0[:, :], xt.ap)
            pr = parts.next()
            act.wait(a, *pr.freed)
            lo = yield from split(bk.ap, pr.ap, SEQ, rest, bk.free)
            park("q", pr, lo, i)
            bk = misc.next()
            pe.wait(*bk.freed)
            for t in range(QT):
                mm(bk.ap[32 * t:32 * t + 32, 0:P], wkv0[:, 0, :], xt.ap[:, t * P:(t + 1) * P])
            for t in range(QT):
                a = mm(bk.ap[:, P + 32 * t:P + 32 * t + 32], xt.ap[:, t * P:(t + 1) * P], wkv0[:, 1, :])
            xt.free(a)
            act.wait(a, *values_free[b % 3])
            values_in[b % 3] = copy_a(values[b % 3][:, :, 0:KV0 * VW].rearrange("p t (g w) -> p t g w", w=VW)[:, :, :, 0:HD],
                                      bk.ap[:, P:2 * P].rearrange("p (t g d) -> p t g d", t=QT, g=KV0))
            pr = parts.next()
            act.wait(*pr.freed)
            lo = yield from split(bk.ap[:, 0:P], pr.ap, P, rest, bk.free)
            park("k", pr, lo, i, P)
            yield

        def rotate(bk0, bk1, ready):
            dve.wait(*ready, *rot[0].freed, *rot[1].freed)
            a = tt(rot[0].ap, bk0.ap, cos_t[:, :], ALU.mult)
            b = tt(rot[1].ap, bk1.ap, sin_t[:, :], ALU.mult)
            bk0.free(a)
            bk1.free(b)
            pool.wait(a, b)
            c = tt(exact.ap, rot[0].ap, rot[1].ap, ALU.add, pool)
            rot[1].freed = [c]
            return c

        def exact_free(*points):
            exact.freed = list(points)

        def front1(b):
            i = b % 2
            dve.wait(*xn.freed)
            a = yield from normalise(b, xn.ap)
            yield
            xt, c, a = transposed_rows(xn.ap, a)
            xn.freed = [a]
            yield
            bk = misc.next()
            pe.wait(got_attention1, c, *bk.freed)
            for t in range(QT):
                a = mm(bk.ap[:, t * LATENT:(t + 1) * LATENT], xt.ap[:, t * P:(t + 1) * P], wdkv[:, :])
            act.wait(a, *lat_n.freed)
            lat = copy_a(lat_n.ap, bk.ap[:, 0:QT * LATENT].rearrange("p (t n) -> p t n", t=QT))
            bk.free(lat)
            yield
            bk0, bk1 = misc.next(), misc.next()
            pe.wait(*bk0.freed, *bk1.freed)
            mm(bk0.ap, wq1[:, :], xt.ap)
            a = mm(bk1.ap, wq1_sw[:, :], xt.ap)
            xt.free(a)
            c = rotate(bk0, bk1, [a, got_attention1])
            yield
            dve.wait(lat)
            s, mv, rs = yield from row_stats(lambda t: lat_n.ap[:, t, :])
            for t in range(QT):
                a = ts(lat_n.ap[:, t, :], lat_n.ap[:, t, :], mv[:, t, 0:1], rs[:, t, :], ALU.subtract, ALU.mult)
            s.free(a)
            dve.wait(a)
            a = tt(lat_n.ap, lat_n.ap, ln_gb[:, 0:1, :].to_broadcast([P, QT, LATENT]), ALU.mult)
            dve.wait(a)
            lat_ready = tt(lat_n.ap, lat_n.ap, ln_gb[:, 1:2, :].to_broadcast([P, QT, LATENT]), ALU.add)
            pr = parts.next()
            act.wait(c, *pr.freed)
            lo = yield from split(exact.ap, pr.ap, SEQ, rest, exact_free)
            park("q", pr, lo, i)
            bk = misc.next()
            pe.wait(lat_ready, *bk.freed)
            for t in range(QT):
                a = transpose(bk.ap[0:LATENT, t * P:(t + 1) * P], lat_n.ap[:, t, :], ident)
            lat_n.freed = [a]
            act.wait(a, *lat_t.freed)
            c = copy_a(lat_t.ap, bk.ap[0:LATENT, :])
            bk.free(c)
            yield
            yield
            bk0, bk1 = misc.next(), misc.next()
            pe.wait(c, *bk0.freed, *bk1.freed)
            mm(bk0.ap, wu1[:, 0, :], lat_t.ap)
            a = mm(bk1.ap, wu1[:, 1, :], lat_t.ap)
            c = rotate(bk0, bk1, [a])
            yield
            bk = misc.next()
            pe.wait(*bk.freed)
            for t in range(QT):
                a = mm(bk.ap[:, t * P:(t + 1) * P], lat_t.ap[:, t * P:(t + 1) * P], wu1[:, 2, :])
            lat_t.freed = [a]
            act.wait(a, *values_free[b % 3])
            values_in[b % 3] = copy_a(values[b % 3][:, :, 0:HEADS * VW].rearrange("p t (h w) -> p t h w", w=VW)[:, :, :, 0:HD],
                                      bk.ap.rearrange("p (t h d) -> p t h d", t=QT, h=HEADS))
            bk.free(values_in[b % 3])
            yield
            pr = parts.next()
            act.wait(c, *pr.freed)
            lo = yield from split(exact.ap, pr.ap, SEQ, rest, exact_free)
            park("k", pr, lo, i)
            yield

        def kv_of(layer, h):
            return h // (HEADS // KV0) if layer == 0 else h

        def maxima(layer, b):
            i = b % 2
            nm = neg_max[i]
            for f in range(2):
                pe.wait(stacked["q", i, f], stacked["k", i, f])
                for t in range(QT):
                    width = (t + 1) * P
                    per = SEQ // width
                    for h0 in range(f * HEADS // 2, (f + 1) * HEADS // 2, per):
                        bk = max_banks.next()
                        pe.wait(*bk.freed)
                        for j in range(per):
                            h = h0 + j
                            mm(bk.ap[:, j * width:(j + 1) * width], q_stack[i][0:MAXROW, h, t * P:(t + 1) * P],
                               k_stack[i][0:MAXROW, kv_of(layer, h), 0:width], stop=False)
                            a = mm(bk.ap[:, (j + 1) * width - P:(j + 1) * width], ident_bf[:, :], mask_bf[:, :], start=False)
                        dve.wait(a, *nm.freed)
                        last = reduce(nm.ap[:, t * HEADS + h0:t * HEADS + h0 + per],
                                      bk.ap[:, 0:per * width].rearrange("p (j n) -> p j n", j=per), ALU.max, negate=True)
                        bk.free(last)
                        yield
            yield
            bk = misc.next()
            pe.wait(last, *bk.freed)
            n = QT * HEADS
            a = transpose(bk.ap[0:n, 0:P], nm.ap, ident)
            nm.freed = [a]
            act.wait(a, *max_parts.freed)
            lo = yield from split(bk.ap[0:n, 0:P], max_parts.ap, P, max_rest, bk.free)
            sp.wait(lo)
            m_parked = dma(park_streams["m", i], max_out[i].rearrange("s p n -> p s n"), max_parts.ap)
            max_parts.freed = [m_parked]
            sp.wait(m_parked, *stack_free[i])
            for t in range(QT):
                maxima_in[i] = dma(stack_streams["m", i], q_stack[i][MAXROW:MAXROW + 3, :, t * P:(t + 1) * P],
                                   max_out[i][:, t * HEADS:(t + 1) * HEADS, :])
            yield

        def prep(layer, b):
            return (front0 if layer == 0 else front1)(b)

        PREP_STEPS = (12, 17)
        MAX_STEPS = 45
        LAG = 2

        waiting, quads_done, projections = [], [], []

        def value_products(layer, b, quad, u, p, masked):
            pe.wait(masked, values_in[b % 3])
            if u == 0:
                pe.wait(*value_bank.freed)
            for j, off in UNITS[u]:
                for c in range(4):
                    col = kv_of(layer, 4 * quad + c) * VW
                    a = mm(value_bank.ap[CW * c:CW * c + CW, j * P:SEQ], values[b % 3][:, j, col:col + CW],
                           p.ap[:, c, off:off + SEQ - j * P], start=(j == 0), stop=(j == QT - 1))
            p.free(a)
            if u == len(UNITS) - 1:
                act.wait(a, *ctx_raw.freed)
                cp = copy_a(ctx_raw.ap, value_bank.ap)
                value_bank.freed = [cp]
                quads_done.append((layer, b, quad, cp))
                if quad == 3:
                    values_free[b % 3] = [a]

        def normalise_quad(layer, b, quad, cp):
            bk = misc.next()
            pe.wait(cp, *bk.freed)
            for t in range(QT):
                a = transpose(bk.ap[:, t * P:(t + 1) * P], ctx_raw.ap[:, t * P:(t + 1) * P], ident)
            ctx_raw.freed = [a]
            v4 = bk.ap.rearrange("p (t c w) -> p t c w", t=QT, c=4)
            dve.wait(a, *ctx_rec.freed)
            r = dve.do(lambda e: e.reciprocal(ctx_rec.ap, v4[:, :, :, HD]))
            dve.wait(r, *ctx_n.freed)
            for t in range(QT):
                r = tt(ctx_n.ap[:, t, 32 * quad:32 * quad + 32].rearrange("p (c d) -> p c d", c=4), v4[:, t, :, 0:HD],
                       ctx_rec.ap[:, t, :].unsqueeze(2).to_broadcast([P, 4, HD]), ALU.mult)
            ctx_rec.freed = [r]
            bk.free(r)
            if quad == 3:
                projections.append(projection(layer, b, r))

        def projection(layer, b, ctx_done):
            wo = wo0 if layer == 0 else wo1
            bk = misc.next()
            pe.wait(ctx_done, *bk.freed)
            for t in range(QT):
                a = transpose(bk.ap[:, t * P:(t + 1) * P], ctx_n.ap[:, t, :], ident)
            ctx_n.freed = [a]
            ctx_t = xn_t.next()
            act.wait(a, *ctx_t.freed)
            c = copy_a(ctx_t.ap, bk.ap)
            bk.free(c)
            yield
            bk = misc.next()
            pe.wait(c, got_attention if layer == 0 else got_attention1, *bk.freed)
            for t in range(QT):
                a = mm(bk.ap[:, t * P:(t + 1) * P], ctx_t.ap[:, t * P:(t + 1) * P], wo[:, :])
            ctx_t.free(a)
            dve.wait(a, x_ready[b])
            rows = X[:, QT * b:QT * b + QT, :]
            r = tt(rows, bk.ap.rearrange("p (t n) -> p t n", t=QT), rows, ALU.add)
            bk.free(r)
            x_ready[b] = r

        def go_on(lag):
            if projections:
                for _ in projections[0]:
                    break
                else:
                    projections.pop(0)
            if quads_done:
                normalise_quad(*quads_done.pop(0))
            if len(waiting) > lag:
                value_products(*waiting.pop(0))

        def core(layer, b):
            i = b % 2
            pe.wait(maxima_in[i])
            for quad in range(4):
                for u, blocks in enumerate(UNITS):
                    p = expd.next()
                    width = blocks[-1][1] + SEQ - blocks[-1][0] * P
                    for c in range(4):
                        h = 4 * quad + c
                        bk = score_banks.next()
                        pe.wait(*bk.freed)
                        for j, off in blocks:
                            a = mm(bk.ap[:, off:off + SEQ - j * P], k_stack[i][:, kv_of(layer, h), j * P:(j + 1) * P],
                                   q_stack[i][:, h, j * P:SEQ])
                        act.wait(a, *p.freed)
                        x = func(p.ap[:, c, 0:width], bk.ap[:, 0:width], ACT.Exp, SCALE)
                        bk.free(x)
                        yield
                    pool.wait(x)
                    if len(blocks) == 1:
                        diag, pat = p.ap[:, :, 0:P], [[0, 4], [1, P]]
                    else:
                        diag = p.ap.rearrange("p c (s n) -> p c s n", n=256)[:, :, :, 0:P]
                        pat = [[0, 4], [0, 2], [1, P]]
                    masked = pool.do(lambda e, diag=diag, pat=pat: e.affine_select(
                        out=diag, in_=diag, compare_op=ALU.is_ge, fill=0.0, base=0, pattern=pat, channel_multiplier=-1))
                    waiting.append((layer, b, quad, u, p, masked))
                    go_on(LAG)
                    yield
            stack_free[i] = [a]
            if b + 2 < BATCHES:
                load_stacks(layer, b + 2)
            if b == BATCHES - 1:
                while waiting or quads_done or projections:
                    go_on(0)
                    yield

        CORE_STEPS = 60

        def after(layer, b):
            yield from route_rows(layer, b)
            if b % GB == GB - 1:
                yield from route(layer, b // GB)

        logits_in = []

        def route_rows(layer, b):
            g4 = b % GB
            dst = xn_half_slots[g4]
            dve.wait(*dst.freed)
            a = yield from normalise(b, dst.ap)
            xn_ready[g4] = a
            yield
            xt, c, _ = transposed_rows(dst.ap, a)
            yield
            yield
            bk = misc.next()
            pe.wait(c, got_attention1, *bk.freed)
            for t in range(QT):
                a = mm(bk.ap[:, t * EXPERTS:(t + 1) * EXPERTS], xt.ap[:, t * P:(t + 1) * P], router[layer][:, :])
            xt.free(a)
            dve.wait(a, got_attention1, *logits.freed)
            r = tt(logits.ap[:, QT * g4:QT * g4 + QT, :], bk.ap[:, 0:QT * EXPERTS].rearrange("p (t e) -> p t e", t=QT),
                   router_b[:, layer:layer + 1, :].to_broadcast([P, QT, EXPERTS]), ALU.add)
            bk.free(r)
            logits_in.append(r)
            yield

        xn_ready = [None] * GB
        route_free = [[], []]
        sent = [[None] * GB, [None] * GB]
        tiles_read = [[], []]
        experts_ready = [None, None]
        gates_ready = [None, None]
        scatter_streams = [Stream(sem(f"scattered{x}")) for x in range(GB)]

        def route(layer, g):
            shape = [P, GT, EXPERTS]

            def wide(ap):
                return ap.unsqueeze(2).to_broadcast(shape)

            def chain(ticket):
                dve.wait(ticket)
                return ticket

            m, total, ksum, vm = (r_small[:, i, :] for i in range(4))
            dve.wait(logits_in[-1], *route_free[g])
            chain(reduce(m, logits.ap, ALU.max))
            a = tt(R[0][:, :, :], logits.ap, wide(m), ALU.subtract)
            logits.freed = [a]
            act.wait(a)
            a = func(R[1][:, :, :], R[0][:, :, :], ACT.Exp)
            chain(a)
            chain(reduce(total, R[1][:, :, :], ALU.add))
            chain(dve.do(lambda e: e.reciprocal(total, total)))
            cur = R[1]
            for k in range(TOPK[layer]):
                chain(reduce(m, cur[:, :, :], ALU.max))
                tt(gates[g][k][:, :], m, total, ALU.mult)
                chain(tt(R[2][:, :, :], cur[:, :, :], wide(m), ALU.is_ge))
                chain(tt(R[3][:, :, :], R[2][:, :, :], consts[:, C_RANK:C_RANK + EXPERTS].unsqueeze(1).to_broadcast(shape), ALU.mult))
                chain(reduce(vm, R[3][:, :, :], ALU.max))
                last = chain(tt(onehot[k][:, :, :], R[3][:, :, :], wide(vm), ALU.is_equal))
                if k + 1 < TOPK[layer]:
                    chain(stt(R[4][:, :, :], onehot[k][:, :, :], -2.0, cur[:, :, :], ALU.mult, ALU.add))
                    cur = R[4]
            gates_ready[g] = last
            by_expert = chosen[:, :, :].rearrange("p e t -> p t e")
            if TOPK[layer] == 1:
                a = copy_v(by_expert, onehot[0][:, :, :])
            else:
                a = tt(by_expert, onehot[0][:, :, :], onehot[1][:, :, :], ALU.add)
            yield
            flat = chosen[:, :, :].rearrange("p e t -> p (e t)")
            bk = misc.next()
            pe.wait(a, *bk.freed)
            n = EXPERTS * GT
            mm(bk.ap[:, 0:n], tri_bf[:, :], flat)
            a = mm(bk.ap[:, n:2 * n], ones_bf[:, :], flat)
            dve.wait(a)

            def et(ap):
                return ap.rearrange("p (e t) -> p e t", e=EXPERTS)

            r0, r2, r3, r5 = (R[i][:, :, :].rearrange("p t e -> p (t e)") for i in (0, 2, 3, 5))
            counts, tiles, cum, base = (e_small[:, i, :] for i in range(4))
            chain(scan(r0, consts[:, C_FIRST:C_FIRST + n], bk.ap[:, n:2 * n]))
            chain(copy_v(counts, et(r0)[:, :, GT - 1]))
            chain(tt(et(r2), counts.unsqueeze(2).to_broadcast([P, EXPERTS, GT]),
                     consts[:, C_THR:C_THR + GT].unsqueeze(1).to_broadcast([P, EXPERTS, GT]), ALU.is_gt))
            chain(reduce(tiles, et(r2), ALU.add))
            chain(scan(cum, consts[:, C_ONE:C_ONE + EXPERTS], tiles))
            chain(tt(base, cum, tiles, ALU.subtract))
            chain(tt(r3, r0, bk.ap[:, n:2 * n], ALU.subtract))
            chain(tt(r5, r3, bk.ap[:, 0:n], ALU.add))
            a = chain(stt(et(r3), base.unsqueeze(2).to_broadcast([P, EXPERTS, GT]), float(P), et(r5), ALU.mult, ALU.add))
            bk.free(a)
            places = et(r3).rearrange("p e t -> p t e")
            for k in range(TOPK[layer]):
                chain(tt(R[2][:, :, :], onehot[k][:, :, :], places, ALU.mult))
                chain(reduce(vm, R[2][:, :, :], ALU.add))
                placed = chain(copy_v(rows_of[g][k][:, :], vm))
            ns = SLOTS[layer]
            sc = slot_cmp[:, 0:ns, :]
            chain(tt(sc, consts[0:1, C_SLOT:C_SLOT + ns].unsqueeze(2).to_broadcast([1, ns, EXPERTS]),
                     cum[0:1, :].unsqueeze(1).to_broadcast([1, ns, EXPERTS]), ALU.is_ge))
            chain(reduce(slot_f[:, 0:ns], sc, ALU.add))
            chain(ts(slot_f[:, 0:ns], slot_f[:, 0:ns], float(EXPERTS - 1), None, ALU.min))
            experts_ready[g] = chain(copy_v(expert_of[g][:, 0:ns], slot_f[:, 0:ns]))
            yield
            places_ready[g] = placed

        places_ready = [None, None]

        def scatter(layer, g, x):
            pool.wait(places_ready[g], filled, xn_ready[x], *tiles_read[g])
            for t in range(QT * x, QT * x + QT):
                for k in range(TOPK[layer]):
                    sent[g][x] = scatter_streams[x].start(pool, lambda e, t=t, k=k: e.indirect_dma_start(
                        sorted_in[g][:, :], bass.IndirectOffsetOnAxis(ap=rows_of[g][k][:, t:t + 1], axis=0),
                        xn_half[:, t, :], None))
                    yield
            xn_half_slots[x].free(sent[g][x])

        SCATTER_STEPS = tuple(QT * k for k in TOPK)

        def load_layer1_experts():
            sp.wait(*weights_free)
            for e in range(EXPERTS):
                dma(load_w, w1[1][:, e, :], d["w1_1"][e])
            dma(load_w, w2[1].rearrange("p e (c n) -> p e c n", c=FCH), d["w2_1"].rearrange("e (c p) n -> p e c n", p=P))
            return dma(load_w, b1_all, d["b1"].rearrange("e n -> (e n)").partition_broadcast(P).rearrange("p (e n) -> p e n", e=EXPERTS))

        weights_free = []
        in_streams = [Stream(sem(f"rows_in{i}")) for i in range(2)]
        out_streams = [Stream(sem(f"rows_out{i}")) for i in range(2)]
        stored = [[], []]
        gathers_done = [[], []]

        def experts(layer, g, got_w):
            ns = SLOTS[layer]
            hb = Ring(bank[0:4])
            tb = misc
            side = (bank[5], bank[6])
            pe.wait(got_w, experts_ready[g])
            dve.wait(got_w)
            tiles_read[g] = []
            group = {}

            def fetch(q):
                n = min(4, ns - 4 * q)
                src = rows_in.next()
                sp.wait(*sent[g], *src.freed)
                got = dma(in_streams[rows_in.at % 2], src.ap[:, 0:n * P].rearrange("p (t n) -> p t n", t=n),
                          sorted_in[g][4 * q * P:(4 * q + n) * P, :].rearrange("(t p) d -> p t d", p=P))
                tiles_read[g] = [got] + tiles_read[g][:1]
                return src, got, n

            def turn(q, src, got, n):
                bk, dst = side[q % 2], rows_t.next()
                pe.wait(got, *bk.freed)
                for t in range(n):
                    a = transpose(bk.ap[:, t * P:(t + 1) * P], src.ap[:, t * P:(t + 1) * P], ident)
                src.free(a)
                act.wait(a, *dst.freed)
                c = copy_a(dst.ap[:, 0:n * P], bk.ap[:, 0:n * P])
                bk.free(c)
                group[q] = [dst, c, rows_out.next(), n, rows_out.at % 2]

            def first(j):
                dst, c = group[j // 4][0:2]
                h = [hb.next() for _ in range(2 - layer)]
                for x in h:
                    pe.wait(*x.freed)
                pe.wait(c)
                reg = {}

                def load(e):
                    reg["e"] = e.value_load(expert_of[g][0:1, j:j + 1], min_val=0, max_val=EXPERTS - 1)

                pe.steps.append((Ticket(pe, len(pe.steps)), load))
                xs = dst.ap[:, (j % 4) * P:(j % 4 + 1) * P]
                for n, x in enumerate(h):
                    a = pe.do(lambda e, n=n, x=x: e.matmul(
                        x.ap, xs, w1[layer][:, bass.ds(reg["e"], 1), n * FFN:(n + 1) * FFN].rearrange("p a n -> p (a n)"),
                        start=True, stop=True))
                dst.free(a)
                hd = hidden.next()
                if layer == 0:
                    s = silu_a.next()
                    act.wait(a, *s.freed)
                    f = func(s.ap, h[0].ap, ACT.Silu)
                    dve.wait(f, *hd.freed)
                    m = tt(hd.ap, h[1].ap, s.ap, ALU.mult)
                    s.free(m)
                    h[0].free(f)
                    h[1].free(m)
                    return reg, hd, m
                dreg = {}

                def dload(e):
                    dreg["e"] = e.value_load(expert_of[g][0:1, j:j + 1], min_val=0, max_val=EXPERTS - 1)

                dve.wait(experts_ready[g])
                dve.steps.append((Ticket(dve, len(dve.steps)), dload))
                dve.wait(a, *hd.freed)
                m = dve.do(lambda e: e.tensor_tensor(hd.ap, h[0].ap, b1_all[:, bass.ds(dreg["e"], 1), :].rearrange("p a n -> p (a n)"), ALU.add))
                h[0].free(m)
                return reg, hd, m, dreg

            def turn_hidden(j, hd, m):
                bk, ht = tb.next(), hidden_t.next()
                pe.wait(m, *bk.freed)
                for c in range(FCH):
                    a = transpose(bk.ap[:, c * P:(c + 1) * P], hd.ap[:, c * P:(c + 1) * P], ident)
                hd.free(a)
                act.wait(a, *ht.freed)
                c = func(ht.ap, bk.ap, ACT.Copy if layer == 0 else ACT.Relu)
                bk.free(c)
                return ht, c

            def second(j, ht, c, reg, dreg):
                q = j // 4
                out, n, slot = group[q][2:5]
                bk = side[q % 2]
                pe.wait(c)
                if j % 4 == 0:
                    pe.wait(*bk.freed)
                cols = slice((j % 4) * P, (j % 4 + 1) * P)
                for k in range(FCH):
                    a = pe.do(lambda e, k=k: e.matmul(
                        bk.ap[:, cols], ht.ap[:, k * P:(k + 1) * P],
                        w2[layer][:, bass.ds(reg["e"], 1), k * DIM:(k + 1) * DIM].rearrange("p a n -> p (a n)"),
                        start=(k == 0), stop=(k == FCH - 1)))
                ht.free(a)
                weights_free[:] = [a]
                group[q][5:] = group[q][5:] + [dreg]
                if j % 4 == n - 1:
                    dve.wait(a, *out.freed)
                    if layer == 0:
                        done = copy_v(out.ap[:, 0:n * P], bk.ap[:, 0:n * P])
                    else:
                        for x, rg in enumerate(group[q][5:]):
                            done = dve.do(lambda e, x=x, rg=rg: e.tensor_tensor(
                                out.ap[:, x * P:(x + 1) * P], bk.ap[:, x * P:(x + 1) * P],
                                b2_all[:, bass.ds(rg["e"], 1), :].rearrange("p a n -> p (a n)"), ALU.add))
                if j % 4 == n - 1:
                    bk.free(done)
                    sp.wait(done, *gathers_done[g])
                    got = dma(out_streams[slot], sorted_out[g][4 * q * P:(4 * q + n) * P, :].rearrange("(t p) d -> p t d", p=P),
                              out.ap[:, 0:n * P].rearrange("p (t n) -> p t n", t=n))
                    out.free(got)
                    stored[g] = [got] + stored[g][:1]

            stored[g] = []
            quads = (ns + 3) // 4
            fetched = {0: fetch(0)}
            f, t = {}, {}
            turn(0, *fetched[0])
            for j in range(ns + 2):
                if j % 4 == 0 and j // 4 + 1 < quads:
                    fetched[j // 4 + 1] = fetch(j // 4 + 1)
                if j < ns:
                    f[j] = first(j)
                if 1 <= j <= ns:
                    t[j - 1] = turn_hidden(j - 1, f[j - 1][1], f[j - 1][2])
                if j >= 2:
                    fj = f[j - 2]
                    second(j - 2, *t[j - 2], fj[0], fj[3] if layer else None)
                if j % 4 == 2 and j // 4 + 1 < quads:
                    turn(j // 4 + 1, *fetched[j // 4 + 1])
                yield

        def combine(layer, g, x):
            pool.wait(*stored[g])
            b = g * GB + x
            for t in range(QT * x, QT * x + QT):
                for k in range(TOPK[layer]):
                    s = gathered.next()
                    pool.wait(*s.freed)
                    got = gather_streams[gathered.at % 4].start(pool, lambda e, t=t, k=k, s=s: e.indirect_dma_start(
                        s.ap[:, :], None, sorted_out[g][0:SLOTS[layer] * P, :], bass.IndirectOffsetOnAxis(ap=rows_of[g][k][:, t:t + 1], axis=0)))
                    dve.wait(got, gates_ready[g], x_ready[b])
                    row = X[:, g * GT + t, :]
                    a = stt(row, s.ap[:, :], gates[g][k][:, t:t + 1], row, ALU.mult, ALU.add)
                    s.free(a)
                    x_ready[b] = a
                    yield
            if layer == 1:
                sp.wait(x_ready[b])
                dma(out_stream, d["out"].rearrange("b (t p) d -> b p t d", p=P)[b], X[:, QT * b:QT * b + QT, :])
            gathers_done[g] = [x_ready[b]]
            route_free[g] = [x_ready[b], *weights_free]

        out_stream = Stream(sem("out_stored"))

        def run(gen):
            for _ in gen:
                pass

        def chain_of(*gens):
            for g in gens:
                yield from g

        def stacks(layer, b):
            load_stacks(layer, b)
            yield

        def prologue(layer):
            return chain_of(prep(layer, 0), stacks(layer, 0), prep(layer, 1), stacks(layer, 1), maxima(layer, 0))

        PROLOGUE_STEPS = tuple(2 * n + 2 + MAX_STEPS for n in PREP_STEPS)
        run(prep(0, 0))
        set_stacks(1, dve)
        pe.wait(*stacks_set[0], *stacks_set[1])
        run(chain_of(stacks(0, 0), prep(0, 1), stacks(0, 1)))
        filled = fill_with_zeros()
        got_w = load_layer0_experts()
        run(maxima(0, 0))
        for layer in range(2):
            for b in range(BATCHES):
                sides = []
                if b > 0:
                    sides.append((after(layer, b - 1), 8, 0.5, 0.95))
                if b + 1 < BATCHES:
                    sides.append((maxima(layer, b + 1), MAX_STEPS, 0.08, 0.75))
                if b + 2 < BATCHES:
                    sides.append((prep(layer, b + 2), PREP_STEPS[layer], 0.0, 0.8))
                if b > GB:
                    done = (b - GB - 1,) if b < BATCHES - 1 else (GB - 2, GB - 1)
                    sides.append((chain_of(*[scatter(layer, 0, x) for x in done]), len(done) * SCATTER_STEPS[layer], 0.0, 0.45 * len(done)))
                if layer == 1 and b < GB:
                    sides.append((combine(0, 1, b), QT, 0.0, 0.6))
                if layer == 1 and b == 1:
                    got_w = load_layer1_experts()
                weave(core(layer, b), CORE_STEPS, *sides)
            shared = []
            for s in expd.slots:
                shared += s.freed
            rings = (rows_in, rows_t, silu_a, hidden, hidden_t, rows_out)
            for r in rings:
                for s in r.slots:
                    s.freed = list(shared)
            weave(experts(layer, 0, got_w), SLOTS[layer] + 2,
                  (chain_of(after(layer, BATCHES - 1), *[scatter(layer, 1, x) for x in range(GB)]),
                   6 + GB * SCATTER_STEPS[layer], 0.0, 0.9))
            sides = [(chain_of(*[combine(layer, 0, x) for x in range(GB)]), GB * SCATTER_STEPS[layer], 0.0, 0.3 + 0.6 * layer)]
            if layer == 0:
                sides.append((prologue(1), PROLOGUE_STEPS[1], 0.3, 1.0))
            weave(experts(layer, 1, got_w), SLOTS[layer] + 2, *sides)
            if layer == 0:
                shared = []
                for r in rings:
                    for s in r.slots:
                        shared += s.freed
                for s in expd.slots:
                    s.freed = list(shared)
        run(chain_of(*[combine(1, 1, x) for x in range(GB)]))
        sp.wait(Landed(out_stream.sem, out_stream.sent))
        for s in out_streams + scatter_streams:
            sp.wait(Landed(s.sem, s.sent))

        for q in (pe, act, dve, pool, sp):
            q.count()

        block = ctx.enter_context(nc.Block())

        @block.sync
        def _(eng):
            sp.emit(eng)

        @block.scalar
        def _(eng):
            act.emit(eng)

        @block.vector
        def _(eng):
            dve.emit(eng)

        @block.gpsimd
        def _(eng):
            pool.emit(eng)

        @block.tensor
        def _(eng):
            pe.emit(eng)


def constants():
    import numpy as np
    c = np.zeros((P, C_ALL), np.float32)
    p = np.arange(P)
    c[:, C_ID:C_ID + P] = np.eye(P)
    masks = np.zeros((P, 2 * P), np.float32)
    masks[:, 0:P] = np.where(p[None, :] > p[:, None], NEG, 0.0)
    masks[:, P:2 * P] = p[:, None] < p[None, :]
    c[:, C_FIRST:C_FIRST + P] = p[None, :] % GT != 0
    c[:, C_ONE:C_ONE + EXPERTS] = 1.0
    c[:, C_RANK:C_RANK + EXPERTS] = EXPERTS - np.arange(EXPERTS)
    c[:, C_THR:C_THR + GT] = P * np.arange(GT)
    c[:, C_SLOT:C_SLOT + MAXSLOTS] = np.arange(MAXSLOTS)
    c[:, C_HALF:C_HALF + QT] = -0.5
    half = HD // 2
    pos = np.arange(SEQ, dtype=np.float32)[:, None]
    inv = (1.0 / 10000.0 ** (np.arange(half, dtype=np.float32) / half)).astype(np.float32)
    ang = (pos * inv[None, :]).astype(np.float32)
    sin, cos = np.sin(ang).T, np.cos(ang).T
    cos_t = np.tile(np.concatenate([cos, cos], 0), (HEADS, 1))
    sin_t = np.tile(np.concatenate([-sin, sin], 0), (HEADS, 1))
    return c, masks, np.ascontiguousarray(cos_t, np.float32), np.ascontiguousarray(sin_t, np.float32)


def kernel(**inputs):
    import numpy as np
    import concourse.bacc as bacc
    from concourse.bass_utils import run_bass_kernel_spmd as launch

    a = {k: np.asarray(v) for k, v in inputs.items()}
    swap = [h * HD + (x + HD // 2) % HD for h in range(HEADS) for x in range(HD)]
    c, masks, cos_t, sin_t = constants()
    arrays = {
        "x": a["L0_attn_x"], "consts": c, "masks": masks, "cos": cos_t, "sin": sin_t,
        "wq0": a["L0_attn_wq"].T, "wk0": a["L0_attn_wk"].T, "wv0": a["L0_attn_wv"].T, "wo0": a["L0_attn_wo"].T,
        "router0": a["L0_ffn_router_w"], "router_b0": a["L0_ffn_router_b"], "w1_0": a["L0_ffn_w1"], "w2_0": a["L0_ffn_w2"],
        "wq1": a["L1_attn_W_q"], "wq1_sw": a["L1_attn_W_q"][:, swap], "wo1": a["L1_attn_W_o"], "wdkv": a["L1_attn_W_dkv"],
        "wuk": a["L1_attn_W_uk"], "wuk_sw": a["L1_attn_W_uk"][:, swap], "wuv": a["L1_attn_W_uv"],
        "ln_gamma": a["L1_attn_ln_gamma"], "ln_beta": a["L1_attn_ln_beta"],
        "router1": a["L1_ffn_gate_w"].T, "router_b1": a["L1_ffn_gate_b"],
        "w1_1": a["L1_ffn_w1"], "b1": a["L1_ffn_b1"], "w2_1": a["L1_ffn_w2"], "b2": a["L1_ffn_b2"],
    }
    arrays = {k: np.ascontiguousarray(v) for k, v in arrays.items()}
    nc = bacc.Bacc("TRN2", target_bir_lowering=False, num_devices=1, dynamic_dma_scratch_size=8192)
    d = {k: nc.dram_tensor(f"in_{k}", v.shape, mybir.dt.from_np(v.dtype), kind="ExternalInput").ap() for k, v in arrays.items()}
    d["out"] = nc.dram_tensor("out_0", (BATCHES, SEQ, DIM), F32, kind="ExternalOutput").ap()
    two_layers(nc, d)
    r = launch(nc, [{f"in_{k}": v for k, v in arrays.items()}], core_ids=[0])
    return r.results[0]["out_0"]
```

```python
import concourse.bass as bass
from concourse import mybir
from contextlib import ExitStack
from itertools import islice

F32 = mybir.dt.float32
BF16 = mybir.dt.bfloat16
I32 = mybir.dt.int32
ALU = mybir.AluOpType
ACT = mybir.ActivationFunctionType
AX = mybir.AxisListType.X

P = 128
BATCHES, SEQ, DIM = 8, 512, 128
QT = SEQ // P
TILES = BATCHES * QT
HEADS, HD = 16, 8
HALF_HEADS = HEADS // 2
KV0 = 4
LATENT = 32
EXPERTS = 8
FFN = 512
FCH = FFN // P
HALVES = 2
GB = BATCHES // HALVES
GT = GB * QT
TOPK = (1, 2)
SLOTS = tuple(GT * k + EXPERTS - 1 for k in TOPK)
MAXSLOTS = max(SLOTS)
EPS = 1e-5
SCALE = float(HD) ** -0.5
NEG = -3.0e38
VW = HD + 1
CW = 32
GROUPS = 6
RUNS_OF_Q = ((0, 3, 0, 0), (3, 2, 1, 0), (5, 1, 2, 0))
RUNS_OF_K = ((0, 3, 0, 1), (3, 2, 0, 1), (5, 1, 0, 0))
MAXROW = 96
UNITS = (((0, 0),), ((1, 0),), ((2, 0), (3, 256)))

C_ID, C_FIRST, C_ONE, C_RANK, C_THR, C_SLOT, C_HALF = 0, 128, 256, 264, 272, 288, 328
C_ALL = 332


class Ticket:

    def __init__(self, queue, at):
        self.queue, self.at, self.used, self.value = queue, at, False, None


class Landed:

    def __init__(self, sem, value):
        self.sem, self.value = sem, value


class Queue:

    def __init__(self, sem):
        self.sem, self.steps, self.seen = sem, [], {}

    def wait(self, *points):
        for p in points:
            if isinstance(p, Landed):
                key, at = id(p.sem), p.value
            else:
                key, at = id(p.queue), p.at
            if self.seen.get(key, -1) < at:
                self.seen[key] = at
                if isinstance(p, Ticket):
                    p.used = True
                self.steps.append(p)

    def do(self, make):
        ticket = Ticket(self, len(self.steps))
        self.steps.append((ticket, make))
        return ticket

    def count(self):
        n = 0
        for s in self.steps:
            if isinstance(s, tuple) and s[0].used:
                n += 1
                s[0].value = n

    def emit(self, eng):
        for s in self.steps:
            if isinstance(s, Landed):
                eng.wait_ge(s.sem, s.value)
            elif isinstance(s, Ticket):
                eng.wait_ge(s.queue.sem, s.value)
            else:
                ins = s[1](eng)
                if s[0].used:
                    ins.then_inc(self.sem, 1)


class Stream:

    def __init__(self, sem):
        self.sem, self.sent = sem, 0

    def start(self, queue, make):
        queue.do(lambda e: make(e).then_inc(self.sem, 16))
        self.sent += 16
        return Landed(self.sem, self.sent)


class Slot:

    def __init__(self, ap):
        self.ap, self.freed, self.taken = ap[:], [], False

    def free(self, *points):
        self.freed, self.taken = list(points), False


class Ring:
    def __init__(self, slots):
        self.slots, self.at = slots, -1

    def next(self):
        self.at += 1
        slot = self.slots[self.at % len(self.slots)]
        assert not slot.taken, "taken again before its readers are in the program"
        slot.taken = True
        return slot


def weave(main, steps, *sides):
    live = [[g, n, a, z, 0] for g, n, a, z in sides]

    def advance(s, upto):
        while s[4] < upto:
            s[4] += 1
            try:
                next(s[0])
            except StopIteration:
                live.remove(s)
                return

    at = 0
    for _ in main:
        at += 1
        for s in list(live):
            if at / steps > s[2]:
                advance(s, s[1] * (at / steps - s[2]) / (s[3] - s[2]))
    for s in list(live):
        advance(s, float("inf"))


def two_layers(nc, d):
    ctx = ExitStack()
    with ctx:
        def sb(name, shape, dt=F32):
            return ctx.enter_context(nc.sbuf_tensor(name, shape, dt))

        def sem(name):
            return ctx.enter_context(nc.semaphore(name))

        pe, act, dve, pool, sp = (Queue(sem(n)) for n in ("pe_done", "act_done", "dve_done", "pool_done", "sp_done"))

        X = sb("X", [P, TILES, DIM])
        consts = sb("consts", [P, C_ALL])
        ident_bf = sb("ident_bf", [P, P], BF16)
        mask_bf = sb("mask_bf", [P, P], BF16)
        tri_bf = sb("tri_bf", [P, P], BF16)
        ones_bf = sb("ones_bf", [P, P], BF16)
        cos_t = sb("cos_t", [P, SEQ])
        sin_t = sb("sin_t", [P, SEQ])
        wq0, wo0 = sb("wq0", [P, P]), sb("wo0", [P, P])
        wkv0 = sb("wkv0", [P, 2, KV0 * HD])
        wq1, wq1_sw, wo1 = sb("wq1", [P, P]), sb("wq1_sw", [P, P]), sb("wo1", [P, P])
        wdkv = sb("wdkv", [P, LATENT])
        wu1 = sb("wu1", [LATENT, 3, P])
        ln_gb = sb("ln_gb", [P, 2, LATENT])
        router = [sb("router0", [P, EXPERTS]), sb("router1", [P, EXPERTS])]
        router_b = sb("router_b", [P, 2, EXPERTS])
        big = sb("expert_weights", [P, EXPERTS * FFN * 3])
        n1, nb = EXPERTS * FFN, EXPERTS * (FFN + FCH)
        w1 = [big[:, 0:2 * n1].rearrange("p (e n) -> p e n", e=EXPERTS),
              big[:, 0:nb].rearrange("p (e n) -> p e n", e=EXPERTS)]
        w2 = [big[:, 2 * n1:3 * n1].rearrange("p (e n) -> p e n", e=EXPERTS),
              big[:, nb:nb + n1].rearrange("p (e n) -> p e n", e=EXPERTS)]
        b2_all = big[:, nb + n1:nb + n1 + EXPERTS * DIM].rearrange("p (e n) -> p e n", e=EXPERTS)
        W1_COLS = (2 * FFN, FFN + FCH)

        q_stack = [sb(f"q_stack{i}", [P, HEADS, SEQ], BF16) for i in range(2)]
        k_stack = [sb(f"k_stack{i}", [P, HEADS, SEQ], BF16) for i in range(2)]
        VROW = HEADS * VW + CW - VW
        values = [sb(f"values{i}", [P, QT, VROW]) for i in range(3)]
        scratch = sb("scratch", [P, 3 * 4 * SEQ])
        scr3 = scratch[:, :].rearrange("p (s c n) -> p s c n", s=3, c=4)
        expd = Ring([Slot(scr3[:, i]) for i in range(3)])
        scr12 = scratch[:, :].rearrange("p (s n) -> p s n", s=12)
        rows_in = Ring([Slot(scr12[:, i]) for i in (0, 1)])
        rows_t = Ring([Slot(scr12[:, i]) for i in (2, 3)])
        silu_a = Ring([Slot(scr12[:, i]) for i in (4, 5)])
        hidden_t = Ring([Slot(scr12[:, i]) for i in (6, 7)])
        rows_out = Ring([Slot(scr12[:, i]) for i in (8, 9)])
        w1_spaces = (scratch[:, 10 * SEQ:12 * SEQ], sb("w1_now", [P, 2 * W1_COLS[1]])[:, :])
        w1_now = (Ring([Slot(x[:, 0:W1_COLS[0]]) for x in w1_spaces]),
                  Ring([Slot(x[:, n:n + W1_COLS[1]]) for x, n in ((w1_spaces[0], 0), (w1_spaces[1], 0), (w1_spaces[1], W1_COLS[1]))]))

        xn_half = sb("xn_half", [P, GT, DIM])
        xn_half_slots = [Slot(xn_half[:, QT * i:QT * i + QT]) for i in range(GB)]
        gathered = Ring([Slot(sb(f"gathered{i}", [P, DIM])) for i in range(4)])
        gather_streams = [Stream(sem(f"gathered_sem{i}")) for i in range(4)]
        xn = Slot(sb("xn", [P, QT, DIM]))
        xn_t = Ring([Slot(sb(f"xn_t{i}", [P, SEQ])) for i in range(3)])
        rot = [Slot(sb(f"rot{i}", [P, SEQ])) for i in range(2)]
        exact, rest = rot
        parts = Ring([Slot(sb("parts", [P, 3, SEQ], BF16))])
        lat_n = Slot(sb("lat_n", [P, QT, LATENT]))
        lat_t = Slot(sb("lat_t", [LATENT, SEQ]))
        neg_max = [Slot(sb(f"neg_max{f}", [P, HALF_HEADS, QT])) for f in range(2)]
        max_parts = Slot(sb("max_parts", [HALF_HEADS * QT, 3, P], BF16))
        max_rest = Slot(sb("max_rest", [HALF_HEADS * QT, P]))
        ctx_raw = Slot(sb("ctx_raw", [P, SEQ]))
        ctx_rec = Slot(sb("ctx_rec", [P, QT, 4]))
        ctx_n = Slot(sb("ctx_n", [P, QT, DIM]))
        ln_small = Ring([Slot(sb(f"ln_small{i}", [P, QT, 10])) for i in range(2)])
        logits = Slot(sb("logits", [P, GT, EXPERTS]))
        R = [sb(f"route{i}", [P, GT, EXPERTS]) for i in range(6)]
        r_small = sb("route_small", [P, 4, GT])
        onehot = [sb(f"onehot{k}", [P, GT, EXPERTS]) for k in range(2)]
        chosen = sb("chosen", [P, EXPERTS, GT], BF16)
        e_small = sb("e_small", [P, 4, EXPERTS])
        slot_cmp = sb("slot_cmp", [1, MAXSLOTS, EXPERTS], BF16)
        slot_f = sb("slot_f", [1, MAXSLOTS])
        gates = [[sb(f"gate{g}{k}", [P, GT]) for k in range(2)] for g in range(HALVES)]
        rows_of = [[sb(f"rows_of{g}{k}", [P, GT], I32) for k in range(2)] for g in range(HALVES)]
        expert_of = [sb(f"expert_of{g}", [1, MAXSLOTS], I32) for g in range(HALVES)]

        psum = ctx.enter_context(nc.psum_tensor("psum", [P, 8, SEQ], F32))
        bank = [Slot(psum[:, i, :]) for i in range(8)]
        max_banks = Ring(bank[0:3])
        score_banks = Ring([bank[3], bank[6]])
        last_score_banks = Ring([bank[3], bank[6]] + bank[0:3])
        value_bank = bank[5]
        misc = Ring([bank[4], bank[7]])

        sorted_in = [nc.dram_tensor(f"sorted_in{g}", (MAXSLOTS * P, DIM), F32, kind="Internal").ap() for g in range(HALVES)]
        sorted_out = [nc.dram_tensor(f"sorted_out{g}", (MAXSLOTS * P, DIM), F32, kind="Internal").ap() for g in range(HALVES)]

        parts_out = {(n, i): nc.dram_tensor(f"{n}_parts{i}", (P, GROUPS, SEQ), BF16, kind="Internal").ap() for n in "qk" for i in range(2)}
        max_out = [nc.dram_tensor(f"max_parts_out{f}", (3, HALF_HEADS * QT, P), BF16, kind="Internal").ap() for f in range(2)]

        ident = consts[:, C_ID:C_ID + P]

        def mm(out, lhsT, rhs, start=True, stop=True):
            return pe.do(lambda e: e.matmul(out, lhsT, rhs, start=start, stop=stop))

        def transpose(out, in_, idn):
            return pe.do(lambda e: e.transpose(out, in_, idn))

        def func(out, in_, f, scale=1.0):
            return act.do(lambda e: e.activation(out, in_, f, scale=scale))

        def copy_a(out, in_):
            return func(out, in_, ACT.Copy)

        def copy_v(out, in_):
            return dve.do(lambda e: e.tensor_copy(out, in_))

        def tt(out, a, b, op, q=dve):
            return q.do(lambda e: e.tensor_tensor(out, a, b, op))

        def ts(out, a, s1, s2, op0, op1=ALU.bypass):
            return dve.do(lambda e: e.tensor_scalar(out, a, s1, s2, op0, op1))

        def stt(out, a, s, b, op0, op1):
            return dve.do(lambda e: e.scalar_tensor_tensor(out=out, in0=a, scalar=s, in1=b, op0=op0, op1=op1))

        def reduce(out, in_, op, negate=False):
            return dve.do(lambda e: e.tensor_reduce(out=out, in_=in_, axis=AX, op=op, negate=negate))

        def scan(out, keep, add):
            return dve.do(lambda e: e.tensor_tensor_scan(out, keep, add, 0.0, ALU.mult, ALU.add))

        def dma(stream, out, in_, q=sp):
            return stream.start(q, lambda e: e.dma_start(out, in_))

        load_x = [Stream(sem(f"load_x{b}")) for b in range(BATCHES)]
        x_ready = [None] * BATCHES
        x_view = d["x"].rearrange("b (t p) d -> b p t d", p=P)
        load_c = Stream(sem("load_consts"))
        load_a = Stream(sem("load_attention_weights"))
        load_w = Stream(sem("load_expert_weights"))

        def load_batch(b):
            x_ready[b] = dma(load_x[b], X[:, QT * b:QT * b + QT, :], x_view[b])

        load_batch(0)
        dma(load_c, consts[:, :], d["consts"])
        got_consts = dma(load_c, scratch[:, 0:2 * P], d["masks"])
        for out, in_ in ((wq0[:, :], d["wq0"]), (wkv0[:, 0, :], d["wk0"]), (wkv0[:, 1, :], d["wv0"]), (wo0[:, :], d["wo0"])):
            got_attention = dma(load_a, out, in_)
        load_batch(1)
        load_a1 = Stream(sem("load_attention1_weights"))
        got_attention1 = Landed(load_a1.sem, 16 * 15)

        def load_rest():
            for b in range(2, BATCHES):
                load_batch(b)
            for out, in_ in ((router[0][:, :], d["router0"]), (router[1][:, :], d["router1"]),
                             (router_b[:, 0, :], d["router_b0"].partition_broadcast(P)),
                             (router_b[:, 1, :], d["router_b1"].partition_broadcast(P)),
                             (wq1[:, :], d["wq1"]), (wq1_sw[:, :], d["wq1_sw"]), (wo1[:, :], d["wo1"]), (wdkv[:, :], d["wdkv"]),
                             (wu1[:, 0, :], d["wuk"]), (wu1[:, 1, :], d["wuk_sw"]), (wu1[:, 2, :], d["wuv"]),
                             (ln_gb[:, 0, :], d["ln_gamma"].partition_broadcast(P)),
                             (ln_gb[:, 1, :], d["ln_beta"].partition_broadcast(P)),
                             (cos_t[:, :], d["cos"]), (sin_t[:, :], d["sin"])):
                got = dma(load_a1, out, in_)
            assert got.value == got_attention1.value

        def load_layer0_expert(e):
            dma(load_w, w1[0][:, e, :], d["w1_0"][e])
            return dma(load_w, w2[0][:, e, :].rearrange("p (c n) -> p c n", c=FCH), d["w2_0"][e].rearrange("(c p) n -> p c n", p=P))

        PAIR_OF_ONES = 1.0 + 0x3F80 / 2.0 ** 23
        stacks_set = [[], []]

        def set_ones(i):
            stacks_set[i].append(dve.do(lambda e: e.memset(k_stack[i][MAXROW:P, :, :].bitcast(F32), PAIR_OF_ONES)))

        def set_zeros(i):
            pool.do(lambda e: e.memset(q_stack[i][:, :, :].bitcast(F32), 0.0))
            stacks_set[i].append(pool.do(lambda e: e.memset(k_stack[i][0:MAXROW, :, :].bitcast(F32), 0.0)))

        def set_values():
            for i in range(3):
                a = pool.do(lambda e, i=i: e.memset(values[i][:, :, :], 1.0))
            act.wait(a)

        set_ones(0)
        dve.wait(got_consts)
        copy_v(ident_bf[:, :], ident)
        copy_v(mask_bf[:, :], scratch[:, 0:P])
        dve.do(lambda e: e.memset(ones_bf[:, :], 1.0))
        bf_ready = copy_v(tri_bf[:, :], scratch[:, P:2 * P])
        for slot in expd.slots:
            slot.freed = [bf_ready]
        for q in (pe, act, pool, sp):
            q.wait(got_consts)
        pe.wait(bf_ready)

        def fill_with_zeros():
            zero_fill = Stream(sem("zero_fill"))
            sp.wait(pool.do(lambda e: e.memset(xn_half[:, :, :], 0.0)))
            for g in range(HALVES):
                for s in range(0, MAXSLOTS, GT):
                    n = min(GT, MAXSLOTS - s)
                    filled = dma(zero_fill, sorted_in[g][s * P:(s + n) * P, :].rearrange("(t p) d -> p t d", p=P), xn_half[:, 0:n, :])
            for s in xn_half_slots:
                s.free(filled)
            return filled

        def row_stats(src):
            s = ln_small.next()
            st, mv, ve, rs = s.ap[:, :, 0:6], s.ap[:, :, 6:8], s.ap[:, :, 8:9], s.ap[:, :, 9:10]
            dve.wait(*s.freed)
            for t in range(QT):
                a = dve.do(lambda e, t=t, rows=src(t): e.bn_stats(st[:, t, :], rows))
            dve.wait(a)
            for t in range(QT):
                a = dve.do(lambda e, t=t: e.bn_aggr(mv[:, t, :], st[:, t, :]))
            dve.wait(a)
            a = ts(ve, mv[:, :, 1:2], EPS, None, ALU.add)
            pool.wait(a)
            a = tt(rs, ve, consts[:, C_HALF:C_HALF + QT].unsqueeze(2), ALU.pow, pool)
            yield
            dve.wait(a)
            return s, mv, rs

        def normalise(b, out):
            dve.wait(x_ready[b])
            s, mv, rs = yield from row_stats(lambda t: X[:, QT * b + t, :])
            for t in range(QT):
                a = ts(out[:, t, :], X[:, QT * b + t, :], mv[:, t, 0:1], rs[:, t, :], ALU.subtract, ALU.mult)
            s.free(a)
            return a

        def transposed_rows(src, ready):
            bk, dst = misc.next(), xn_t.next()
            pe.wait(ready, *bk.freed)
            for t in range(QT):
                a = transpose(bk.ap[:, t * P:(t + 1) * P], src[:, t, :], ident)
            act.wait(a, *dst.freed)
            c = copy_a(dst.ap, bk.ap)
            bk.free(c)
            return dst, c, a

        def split(src, dst, n, rest_slot, release):
            hi = copy_a(dst[:, 0, 0:n], src)
            dve.wait(hi, *rest_slot.freed)
            r = tt(rest_slot.ap[:, 0:n], src, dst[:, 0, 0:n], ALU.subtract)
            release(r, hi)
            yield
            act.wait(r)
            mid = copy_a(dst[:, 1, 0:n], rest_slot.ap[:, 0:n])
            yield
            pool.wait(mid)
            lo = tt(dst[:, 2, 0:n], rest_slot.ap[:, 0:n], dst[:, 1, 0:n], ALU.subtract, pool)
            rest_slot.freed = [lo]
            yield
            return lo

        stack_streams = {(n, i, f): Stream(sem(f"{n}_stacked{i}{f}")) for n in "qkm" for i in range(2) for f in range(2)}
        stack_free = [[], []]
        values_free = [[], [], []]
        stacked = {}
        maxima_in = {}
        values_in = [None, None, None]

        park_streams = {(n, i): Stream(sem(f"{n}_parked{i}")) for n in "qkm" for i in range(2)}

        def park(which, pr, ready, i, n=SEQ):
            out = parts_out[which, i]
            sp.wait(ready)
            for row, rows, part, step in (RUNS_OF_Q if which == "q" else RUNS_OF_K):
                def run_of(ap):
                    return ap[:, part:part + rows, :] if step else ap[:, part:part + 1, :].to_broadcast([ap.shape[0], rows, n])
                if n == SEQ:
                    parked[which, i] = dma(park_streams[which, i], out[:, row:row + rows, :], run_of(pr.ap))
                    continue
                for t in range(QT):
                    parked[which, i] = dma(park_streams[which, i], out[0:KV0 * HD, row:row + rows, t * P:(t + 1) * P],
                                           run_of(pr.ap[32 * t:32 * t + 32, :, 0:n]))
            pr.free(parked[which, i])

        parked = {}

        def load_stacks(layer, b):
            i = b % 2
            for f in range(2):
                for which, dst in (("k", k_stack[i]), ("q", q_stack[i])):
                    heads = (KV0 if layer == 0 and which == "k" else HEADS) // 2
                    sp.wait(parked[which, i], *stacks_set[i], *stack_free[i])
                    stacked[which, i, f] = dma(
                        stack_streams[which, i, f], dst[0:GROUPS * HD, f * heads:(f + 1) * heads, :],
                        parts_out[which, i][f * heads * HD:(f + 1) * heads * HD].rearrange("(h d) r n -> (d r) h n", d=HD))
            parked.pop(("q", i))
            parked.pop(("k", i))

        def front0(b):
            i = b % 2
            dve.wait(*xn.freed)
            a = yield from normalise(b, xn.ap)
            yield
            xt, c, a = transposed_rows(xn.ap, a)
            xn.freed = [a]
            yield
            yield
            bk = misc.next()
            pe.wait(got_attention, c, *bk.freed)
            a = mm(bk.ap, wq0[:, :], xt.ap)
            pr = parts.next()
            act.wait(a, *pr.freed)
            lo = yield from split(bk.ap, pr.ap, SEQ, rest, bk.free)
            park("q", pr, lo, i)
            bk = misc.next()
            pe.wait(*bk.freed)
            for t in range(QT):
                mm(bk.ap[32 * t:32 * t + 32, 0:P], wkv0[:, 0, :], xt.ap[:, t * P:(t + 1) * P])
            for t in range(QT):
                a = mm(bk.ap[:, P + 32 * t:P + 32 * t + 32], xt.ap[:, t * P:(t + 1) * P], wkv0[:, 1, :])
            xt.free(a)
            act.wait(a, *values_free[b % 3])
            values_in[b % 3] = copy_a(values[b % 3][:, :, 0:KV0 * VW].rearrange("p t (g w) -> p t g w", w=VW)[:, :, :, 0:HD],
                                      bk.ap[:, P:2 * P].rearrange("p (t g d) -> p t g d", t=QT, g=KV0))
            pr = parts.next()
            act.wait(*pr.freed)
            lo = yield from split(bk.ap[:, 0:P], pr.ap, P, rest, bk.free)
            park("k", pr, lo, i, P)
            yield

        def rotate(bk0, bk1, ready):
            dve.wait(*ready, *rot[0].freed, *rot[1].freed)
            a = tt(rot[0].ap, bk0.ap, cos_t[:, :], ALU.mult)
            b = tt(rot[1].ap, bk1.ap, sin_t[:, :], ALU.mult)
            bk0.free(a)
            bk1.free(b)
            pool.wait(a, b)
            c = tt(exact.ap, rot[0].ap, rot[1].ap, ALU.add, pool)
            rot[1].freed = [c]
            return c

        def exact_free(*points):
            exact.freed = list(points)

        def front1(b):
            i = b % 2
            dve.wait(*xn.freed)
            a = yield from normalise(b, xn.ap)
            yield
            xt, c, a = transposed_rows(xn.ap, a)
            xn.freed = [a]
            yield
            bk = misc.next()
            pe.wait(got_attention1, c, *bk.freed)
            for t in range(QT):
                a = mm(bk.ap[:, t * LATENT:(t + 1) * LATENT], xt.ap[:, t * P:(t + 1) * P], wdkv[:, :])
            act.wait(a, *lat_n.freed)
            lat = copy_a(lat_n.ap, bk.ap[:, 0:QT * LATENT].rearrange("p (t n) -> p t n", t=QT))
            bk.free(lat)
            yield
            bk0, bk1 = misc.next(), misc.next()
            pe.wait(*bk0.freed, *bk1.freed)
            mm(bk0.ap, wq1[:, :], xt.ap)
            a = mm(bk1.ap, wq1_sw[:, :], xt.ap)
            xt.free(a)
            c = rotate(bk0, bk1, [a, got_attention1])
            yield
            dve.wait(lat)
            s, mv, rs = yield from row_stats(lambda t: lat_n.ap[:, t, :])
            for t in range(QT):
                a = ts(lat_n.ap[:, t, :], lat_n.ap[:, t, :], mv[:, t, 0:1], rs[:, t, :], ALU.subtract, ALU.mult)
            s.free(a)
            dve.wait(a)
            a = tt(lat_n.ap, lat_n.ap, ln_gb[:, 0:1, :].to_broadcast([P, QT, LATENT]), ALU.mult)
            dve.wait(a)
            lat_ready = tt(lat_n.ap, lat_n.ap, ln_gb[:, 1:2, :].to_broadcast([P, QT, LATENT]), ALU.add)
            pr = parts.next()
            act.wait(c, *pr.freed)
            lo = yield from split(exact.ap, pr.ap, SEQ, rest, exact_free)
            park("q", pr, lo, i)
            bk = misc.next()
            pe.wait(lat_ready, *bk.freed)
            for t in range(QT):
                a = transpose(bk.ap[0:LATENT, t * P:(t + 1) * P], lat_n.ap[:, t, :], ident)
            lat_n.freed = [a]
            act.wait(a, *lat_t.freed)
            c = copy_a(lat_t.ap, bk.ap[0:LATENT, :])
            bk.free(c)
            yield
            yield
            bk0, bk1 = misc.next(), misc.next()
            pe.wait(c, *bk0.freed, *bk1.freed)
            mm(bk0.ap, wu1[:, 0, :], lat_t.ap)
            a = mm(bk1.ap, wu1[:, 1, :], lat_t.ap)
            c = rotate(bk0, bk1, [a])
            yield
            bk = misc.next()
            pe.wait(*bk.freed)
            for t in range(QT):
                a = mm(bk.ap[:, t * P:(t + 1) * P], lat_t.ap[:, t * P:(t + 1) * P], wu1[:, 2, :])
            lat_t.freed = [a]
            act.wait(a, *values_free[b % 3])
            values_in[b % 3] = copy_a(values[b % 3][:, :, 0:HEADS * VW].rearrange("p t (h w) -> p t h w", w=VW)[:, :, :, 0:HD],
                                      bk.ap.rearrange("p (t h d) -> p t h d", t=QT, h=HEADS))
            bk.free(values_in[b % 3])
            yield
            pr = parts.next()
            act.wait(c, *pr.freed)
            lo = yield from split(exact.ap, pr.ap, SEQ, rest, exact_free)
            park("k", pr, lo, i)
            yield

        def kv_of(layer, h):
            return h // (HEADS // KV0) if layer == 0 else h

        def maxima(layer, b, f):
            i = b % 2
            nm = neg_max[f]
            pe.wait(stacked["q", i, f], stacked["k", i, f])
            for t in range(QT):
                width = (t + 1) * P
                per = SEQ // width
                for h0 in range(0, HALF_HEADS, per):
                    n = min(per, HALF_HEADS - h0)
                    bk = max_banks.next()
                    pe.wait(*bk.freed)
                    for j in range(n):
                        h = f * HALF_HEADS + h0 + j
                        mm(bk.ap[:, j * width:(j + 1) * width], q_stack[i][0:MAXROW, h, t * P:(t + 1) * P],
                           k_stack[i][0:MAXROW, kv_of(layer, h), 0:width], stop=False)
                        a = mm(bk.ap[:, (j + 1) * width - P:(j + 1) * width], ident_bf[:, :], mask_bf[:, :], start=False)
                    dve.wait(a, *nm.freed)
                    last = reduce(nm.ap[:, h0:h0 + n, t], bk.ap[:, 0:n * width].rearrange("p (j n) -> p j n", j=n),
                                  ALU.max, negate=True)
                    bk.free(last)
                    yield
            bk = misc.next()
            pe.wait(last, *bk.freed)
            n = HALF_HEADS * QT
            a = transpose(bk.ap[0:n, 0:P], nm.ap.rearrange("p h t -> p (h t)"), ident)
            nm.freed = [a]
            act.wait(a, *max_parts.freed)
            lo = yield from split(bk.ap[0:n, 0:P], max_parts.ap, P, max_rest, bk.free)
            sp.wait(lo)
            m_parked = dma(park_streams["m", f], max_out[f].rearrange("s p n -> p s n"), max_parts.ap)
            max_parts.freed = [m_parked]
            sp.wait(m_parked, *stack_free[i])
            maxima_in[i, f] = dma(stack_streams["m", i, f],
                                  q_stack[i][MAXROW:MAXROW + 3, f * HALF_HEADS:(f + 1) * HALF_HEADS, :],
                                  max_out[f].rearrange("s (h t) n -> s h (t n)", t=QT))
            yield

        def prep(layer, b):
            return (front0 if layer == 0 else front1)(b)

        PREP_STEPS = (12, 17)
        MAX_STEPS = sum(-(-HALF_HEADS // (QT // (t + 1))) for t in range(QT)) + 3
        LAG = 2

        waiting, quads_done, projections = [], [], []

        def value_products(layer, b, quad, u, p, masked):
            pe.wait(masked, values_in[b % 3])
            if u == 0:
                pe.wait(*value_bank.freed)
            for j, off in UNITS[u]:
                for c in range(4):
                    col = kv_of(layer, 4 * quad + c) * VW
                    a = mm(value_bank.ap[CW * c:CW * c + CW, j * P:SEQ], values[b % 3][:, j, col:col + CW],
                           p.ap[:, c, off:off + SEQ - j * P], start=(j == 0), stop=(j == QT - 1))
            p.free(a)
            if u == len(UNITS) - 1:
                act.wait(a, *ctx_raw.freed)
                cp = copy_a(ctx_raw.ap, value_bank.ap)
                value_bank.freed = [cp]
                quads_done.append((layer, b, quad, cp))
                if quad == 3:
                    values_free[b % 3] = [a]

        def normalise_quad(layer, b, quad, cp):
            bk = misc.next()
            pe.wait(cp, *bk.freed)
            for t in range(QT):
                a = transpose(bk.ap[:, t * P:(t + 1) * P], ctx_raw.ap[:, t * P:(t + 1) * P], ident)
            ctx_raw.freed = [a]
            v4 = bk.ap.rearrange("p (t c w) -> p t c w", t=QT, c=4)
            dve.wait(a, *ctx_rec.freed)
            r = dve.do(lambda e: e.reciprocal(ctx_rec.ap, v4[:, :, :, HD]))
            dve.wait(r, *ctx_n.freed)
            for t in range(QT):
                r = tt(ctx_n.ap[:, t, 32 * quad:32 * quad + 32].rearrange("p (c d) -> p c d", c=4), v4[:, t, :, 0:HD],
                       ctx_rec.ap[:, t, :].unsqueeze(2).to_broadcast([P, 4, HD]), ALU.mult)
            ctx_rec.freed = [r]
            bk.free(r)
            if quad == 3:
                projections.append(projection(layer, b, r))

        def projection(layer, b, ctx_done):
            wo = wo0 if layer == 0 else wo1
            bk = misc.next()
            pe.wait(ctx_done, *bk.freed)
            for t in range(QT):
                a = transpose(bk.ap[:, t * P:(t + 1) * P], ctx_n.ap[:, t, :], ident)
            ctx_n.freed = [a]
            ctx_t = xn_t.next()
            act.wait(a, *ctx_t.freed)
            c = copy_a(ctx_t.ap, bk.ap)
            bk.free(c)
            yield
            bk = misc.next()
            pe.wait(c, got_attention if layer == 0 else got_attention1, *bk.freed)
            for t in range(QT):
                a = mm(bk.ap[:, t * P:(t + 1) * P], ctx_t.ap[:, t * P:(t + 1) * P], wo[:, :])
            ctx_t.free(a)
            dve.wait(a, x_ready[b])
            rows = X[:, QT * b:QT * b + QT, :]
            r = tt(rows, bk.ap.rearrange("p (t n) -> p t n", t=QT), rows, ALU.add)
            bk.free(r)
            x_ready[b] = r

        def go_on(lag):
            if projections:
                for _ in projections[0]:
                    break
                else:
                    projections.pop(0)
            if quads_done:
                normalise_quad(*quads_done.pop(0))
            if len(waiting) > lag:
                value_products(*waiting.pop(0))

        def core(layer, b):
            i = b % 2
            for quad in range(4):
                pe.wait(maxima_in[i, quad // 2])
                for u, blocks in enumerate(UNITS):
                    p = expd.next()
                    width = blocks[-1][1] + SEQ - blocks[-1][0] * P
                    ring = last_score_banks if b == BATCHES - 1 and quad >= 2 else score_banks
                    for c in range(4):
                        h = 4 * quad + c
                        bk = ring.next()
                        pe.wait(*bk.freed)
                        for j, off in blocks:
                            a = mm(bk.ap[:, off:off + SEQ - j * P], k_stack[i][:, kv_of(layer, h), j * P:(j + 1) * P],
                                   q_stack[i][:, h, j * P:SEQ])
                        act.wait(a, *p.freed)
                        x = func(p.ap[:, c, 0:width], bk.ap[:, 0:width], ACT.Exp, SCALE)
                        bk.free(x)
                        yield
                    pool.wait(x)
                    if len(blocks) == 1:
                        diag, pat = p.ap[:, :, 0:P], [[0, 4], [1, P]]
                    else:
                        diag = p.ap.rearrange("p c (s n) -> p c s n", n=256)[:, :, :, 0:P]
                        pat = [[0, 4], [0, 2], [1, P]]
                    masked = pool.do(lambda e, diag=diag, pat=pat: e.affine_select(
                        out=diag, in_=diag, compare_op=ALU.is_ge, fill=0.0, base=0, pattern=pat, channel_multiplier=-1))
                    waiting.append((layer, b, quad, u, p, masked))
                    go_on(LAG)
                    yield
            stack_free[i] = [a]
            if b + 2 < BATCHES:
                load_stacks(layer, b + 2)
            if b == BATCHES - 1:
                while waiting or quads_done or projections:
                    go_on(0)
                    yield

        CORE_STEPS = 60

        def after(layer, b):
            yield from route_rows(layer, b)
            if b % GB == GB - 1:
                yield from route(layer, b // GB)

        logits_in = []

        def route_rows(layer, b):
            g4 = b % GB
            dst = xn_half_slots[g4]
            dve.wait(*dst.freed)
            a = yield from normalise(b, dst.ap)
            xn_ready[g4] = a
            yield
            xt, c, _ = transposed_rows(dst.ap, a)
            yield
            yield
            bk = misc.next()
            pe.wait(c, got_attention1, *bk.freed)
            for t in range(QT):
                a = mm(bk.ap[:, t * EXPERTS:(t + 1) * EXPERTS], xt.ap[:, t * P:(t + 1) * P], router[layer][:, :])
            xt.free(a)
            dve.wait(a, got_attention1, *logits.freed)
            r = tt(logits.ap[:, QT * g4:QT * g4 + QT, :], bk.ap[:, 0:QT * EXPERTS].rearrange("p (t e) -> p t e", t=QT),
                   router_b[:, layer:layer + 1, :].to_broadcast([P, QT, EXPERTS]), ALU.add)
            bk.free(r)
            logits_in.append(r)
            yield

        xn_ready = [None] * GB
        route_free = [[], []]
        sent = [[None] * GB, [None] * GB]
        tiles_read = [[], []]
        experts_ready = [None, None]
        gates_ready = [None, None]
        scatter_streams = [Stream(sem(f"scattered{x}")) for x in range(GB)]

        def route(layer, g):
            shape = [P, GT, EXPERTS]

            def wide(ap):
                return ap.unsqueeze(2).to_broadcast(shape)

            def chain(ticket):
                dve.wait(ticket)
                return ticket

            m, total, ksum, vm = (r_small[:, i, :] for i in range(4))
            dve.wait(logits_in[-1], *route_free[g])
            chain(reduce(m, logits.ap, ALU.max))
            a = tt(R[0][:, :, :], logits.ap, wide(m), ALU.subtract)
            logits.freed = [a]
            act.wait(a)
            a = func(R[1][:, :, :], R[0][:, :, :], ACT.Exp)
            chain(a)
            chain(reduce(total, R[1][:, :, :], ALU.add))
            chain(dve.do(lambda e: e.reciprocal(total, total)))
            cur = R[1]
            for k in range(TOPK[layer]):
                chain(reduce(m, cur[:, :, :], ALU.max))
                tt(gates[g][k][:, :], m, total, ALU.mult)
                chain(tt(R[2][:, :, :], cur[:, :, :], wide(m), ALU.is_ge))
                chain(tt(R[3][:, :, :], R[2][:, :, :], consts[:, C_RANK:C_RANK + EXPERTS].unsqueeze(1).to_broadcast(shape), ALU.mult))
                chain(reduce(vm, R[3][:, :, :], ALU.max))
                last = chain(tt(onehot[k][:, :, :], R[3][:, :, :], wide(vm), ALU.is_equal))
                if k + 1 < TOPK[layer]:
                    chain(stt(R[4][:, :, :], onehot[k][:, :, :], -2.0, cur[:, :, :], ALU.mult, ALU.add))
                    cur = R[4]
            gates_ready[g] = last
            by_expert = chosen[:, :, :].rearrange("p e t -> p t e")
            if TOPK[layer] == 1:
                a = copy_v(by_expert, onehot[0][:, :, :])
            else:
                a = tt(by_expert, onehot[0][:, :, :], onehot[1][:, :, :], ALU.add)
            yield
            flat = chosen[:, :, :].rearrange("p e t -> p (e t)")
            bk = misc.next()
            pe.wait(a, *bk.freed)
            n = EXPERTS * GT
            mm(bk.ap[:, 0:n], tri_bf[:, :], flat)
            a = mm(bk.ap[:, n:2 * n], ones_bf[:, :], flat)
            dve.wait(a)

            def et(ap):
                return ap.rearrange("p (e t) -> p e t", e=EXPERTS)

            r0, r2, r3, r5 = (R[i][:, :, :].rearrange("p t e -> p (t e)") for i in (0, 2, 3, 5))
            counts, tiles, cum, base = (e_small[:, i, :] for i in range(4))
            chain(scan(r0, consts[:, C_FIRST:C_FIRST + n], bk.ap[:, n:2 * n]))
            chain(copy_v(counts, et(r0)[:, :, GT - 1]))
            chain(tt(et(r2), counts.unsqueeze(2).to_broadcast([P, EXPERTS, GT]),
                     consts[:, C_THR:C_THR + GT].unsqueeze(1).to_broadcast([P, EXPERTS, GT]), ALU.is_gt))
            chain(reduce(tiles, et(r2), ALU.add))
            chain(scan(cum, consts[:, C_ONE:C_ONE + EXPERTS], tiles))
            chain(tt(base, cum, tiles, ALU.subtract))
            chain(tt(r3, r0, bk.ap[:, n:2 * n], ALU.subtract))
            chain(tt(r5, r3, bk.ap[:, 0:n], ALU.add))
            a = chain(stt(et(r3), base.unsqueeze(2).to_broadcast([P, EXPERTS, GT]), float(P), et(r5), ALU.mult, ALU.add))
            bk.free(a)
            places = et(r3).rearrange("p e t -> p t e")
            for k in range(TOPK[layer]):
                chain(tt(R[2][:, :, :], onehot[k][:, :, :], places, ALU.mult))
                chain(reduce(vm, R[2][:, :, :], ALU.add))
                placed = chain(copy_v(rows_of[g][k][:, :], vm))
            ns = SLOTS[layer]
            sc = slot_cmp[:, 0:ns, :]
            chain(tt(sc, consts[0:1, C_SLOT:C_SLOT + ns].unsqueeze(2).to_broadcast([1, ns, EXPERTS]),
                     cum[0:1, :].unsqueeze(1).to_broadcast([1, ns, EXPERTS]), ALU.is_ge))
            chain(reduce(slot_f[:, 0:ns], sc, ALU.add))
            chain(ts(slot_f[:, 0:ns], slot_f[:, 0:ns], float(EXPERTS - 1), None, ALU.min))
            experts_ready[g] = chain(copy_v(expert_of[g][:, 0:ns], slot_f[:, 0:ns]))
            yield
            places_ready[g] = placed

        places_ready = [None, None]

        def scatter(layer, g, x):
            pool.wait(places_ready[g], filled, xn_ready[x], *tiles_read[g])
            for t in range(QT * x, QT * x + QT):
                for k in range(TOPK[layer]):
                    sent[g][x] = scatter_streams[x].start(pool, lambda e, t=t, k=k: e.indirect_dma_start(
                        sorted_in[g][:, :], bass.IndirectOffsetOnAxis(ap=rows_of[g][k][:, t:t + 1], axis=0),
                        xn_half[:, t, :], None))
                    yield
            xn_half_slots[x].free(sent[g][x])

        SCATTER_STEPS = tuple(QT * k for k in TOPK)

        def load_layer1_expert(e):
            sp.wait(*weights_free)
            dma(load_w, w1[1][:, e, 0:FFN], d["w1_1"][e])
            dma(load_w, w1[1][:, e, FFN:FFN + FCH], d["b1_t"][e])
            dma(load_w, b2_all[:, e, :], d["b2"][e].partition_broadcast(P))
            return dma(load_w, w2[1][:, e, :].rearrange("p (c n) -> p c n", c=FCH), d["w2_1"][e].rearrange("(c p) n -> p c n", p=P))

        weights_free = []
        in_streams = [Stream(sem(f"rows_in{i}")) for i in range(2)]
        out_streams = [Stream(sem(f"rows_out{i}")) for i in range(2)]
        stored = [[], []]
        gathers_done = [[], []]

        BEHIND = 2

        def experts(layer, g, got_w):
            ns = SLOTS[layer]
            hb = Ring(bank[0:4])
            side = (bank[5], bank[6])
            pe.wait(got_w, experts_ready[g])
            dve.wait(got_w)
            tiles_read[g] = []
            group = {}

            def fetch(q):
                n = min(4, ns - 4 * q)
                src = rows_in.next()
                sp.wait(*sent[g], *src.freed)
                got = dma(in_streams[rows_in.at % 2], src.ap[:, 0:n * P].rearrange("p (t n) -> p t n", t=n),
                          sorted_in[g][4 * q * P:(4 * q + n) * P, :].rearrange("(t p) d -> p t d", p=P))
                tiles_read[g] = [got] + tiles_read[g][:1]
                return src, got, n

            def turn(q, src, got, n):
                bk, dst = side[q % 2], rows_t.next()
                pe.wait(got, *bk.freed)
                for t in range(n):
                    a = transpose(bk.ap[:, t * P:(t + 1) * P], src.ap[:, t * P:(t + 1) * P], ident)
                src.free(a)
                act.wait(a, *dst.freed)
                c = copy_a(dst.ap[:, 0:n * P], bk.ap[:, 0:n * P])
                bk.free(c)
                group[q] = [dst, c, rows_out.next(), n, rows_out.at % 2]

            def register(q, j):
                reg = {}

                def load(e):
                    reg["e"] = e.value_load(expert_of[g][0:1, j:j + 1], min_val=0, max_val=EXPERTS - 1)

                q.wait(experts_ready[g])
                q.steps.append((Ticket(q, len(q.steps)), load))
                return reg

            def copy_w1(j):
                w = w1_now[layer].next()
                regs = [register(q, j) for q in (pe, dve)]
                n = 0
                points = []
                if layer == 0:
                    n, areg = FFN, register(act, j)
                    act.wait(got_w, *w.freed)
                    points.append(act.do(lambda e: e.activation(
                        w.ap[:, 0:n], w1[0][:, bass.ds(areg["e"], 1), 0:n].rearrange("p a n -> p (a n)"), ACT.Copy)))
                dve.wait(*w.freed)
                points.append(dve.do(lambda e: e.tensor_copy(
                    w.ap[:, n:W1_COLS[layer]], w1[layer][:, bass.ds(regs[1]["e"], 1), n:W1_COLS[layer]].rearrange("p a n -> p (a n)"))))
                copied[j] = (regs[0], w, points, regs[1])

            def first(j):
                dst, c = group[j // 4][0:2]
                h = [hb.next() for _ in range(2 - layer)]
                for x in h:
                    pe.wait(*x.freed)
                pe.wait(c)
                reg, w, points, dreg = copied.pop(j)
                pe.wait(*points)

                xs = dst.ap[:, (j % 4) * P:(j % 4 + 1) * P]
                for n, x in enumerate(h):
                    for c in range(FCH):
                        a = mm(x.ap[:, c * P:(c + 1) * P], w.ap[:, n * FFN + c * P:n * FFN + (c + 1) * P], xs)
                dst.free(a)
                ht = hidden_t.next()
                if layer == 0:
                    w.free(a)
                    s = silu_a.next()
                    act.wait(a, *s.freed)
                    f = func(s.ap, h[0].ap, ACT.Silu)
                    dve.wait(f, *ht.freed)
                    m = tt(ht.ap, h[1].ap, s.ap, ALU.mult)
                    s.free(m)
                    h[0].free(f)
                    h[1].free(m)
                    return reg, ht, m, dreg
                act.wait(a, points[0], *ht.freed)
                for c in range(FCH):
                    f = act.do(lambda e, c=c: e.activation(ht.ap[:, c * P:(c + 1) * P], h[0].ap[:, c * P:(c + 1) * P], ACT.Relu,
                                                           bias=w.ap[:, FFN + c:FFN + c + 1]))
                h[0].free(f)
                w.free(f)
                return reg, ht, f, dreg

            def second(j, ht, c, reg, dreg):
                q = j // 4
                out, n, slot = group[q][2:5]
                bk = side[q % 2]
                pe.wait(c)
                if j % 4 == 0:
                    pe.wait(*bk.freed)
                cols = slice((j % 4) * P, (j % 4 + 1) * P)
                for k in range(FCH):
                    a = pe.do(lambda e, k=k: e.matmul(
                        bk.ap[:, cols], ht.ap[:, k * P:(k + 1) * P],
                        w2[layer][:, bass.ds(reg["e"], 1), k * DIM:(k + 1) * DIM].rearrange("p a n -> p (a n)"),
                        start=(k == 0), stop=(k == FCH - 1)))
                ht.free(a)
                weights_free[:] = [a]
                group[q][5:] = group[q][5:] + [dreg]
                if j % 4 == n - 1:
                    dve.wait(a, *out.freed)
                    if layer == 0:
                        done = copy_v(out.ap[:, 0:n * P], bk.ap[:, 0:n * P])
                    else:
                        for x, rg in enumerate(group[q][5:]):
                            done = dve.do(lambda e, x=x, rg=rg: e.tensor_tensor(
                                out.ap[:, x * P:(x + 1) * P], bk.ap[:, x * P:(x + 1) * P],
                                b2_all[:, bass.ds(rg["e"], 1), :].rearrange("p a n -> p (a n)"), ALU.add))
                if j % 4 == n - 1:
                    bk.free(done)
                    sp.wait(done, *gathers_done[g])
                    got = dma(out_streams[slot], sorted_out[g][4 * q * P:(4 * q + n) * P, :].rearrange("(t p) d -> p t d", p=P),
                              out.ap[:, 0:n * P].rearrange("p (t n) -> p t n", t=n))
                    out.free(got)
                    stored[g] = [got] + stored[g][:1]

            stored[g] = []
            quads = (ns + 3) // 4
            fetched = {0: fetch(0)}
            f, copied = {}, {}
            ahead = len(w1_now[layer].slots) // 2
            for j in range(ahead):
                copy_w1(j)
            turn(0, *fetched[0])
            for j in range(ns + BEHIND):
                if j % 4 == 0 and j // 4 + 1 < quads:
                    fetched[j // 4 + 1] = fetch(j // 4 + 1)
                if j >= BEHIND:
                    reg, ht, ready, dreg = f.pop(j - BEHIND)
                    second(j - BEHIND, ht, ready, reg, dreg)
                if j + ahead < ns:
                    copy_w1(j + ahead)
                if j < ns:
                    f[j] = first(j)
                if j % 4 == 2 and j // 4 + 1 < quads:
                    turn(j // 4 + 1, *fetched[j // 4 + 1])
                yield

        def combine(layer, g, x):
            pool.wait(*stored[g])
            b = g * GB + x
            for t in range(QT * x, QT * x + QT):
                for k in range(TOPK[layer]):
                    s = gathered.next()
                    pool.wait(*s.freed)
                    got = gather_streams[gathered.at % 4].start(pool, lambda e, t=t, k=k, s=s: e.indirect_dma_start(
                        s.ap[:, :], None, sorted_out[g][0:SLOTS[layer] * P, :], bass.IndirectOffsetOnAxis(ap=rows_of[g][k][:, t:t + 1], axis=0)))
                    dve.wait(got, gates_ready[g], x_ready[b])
                    row = X[:, g * GT + t, :]
                    a = stt(row, s.ap[:, :], gates[g][k][:, t:t + 1], row, ALU.mult, ALU.add)
                    s.free(a)
                    x_ready[b] = a
                    yield
            if layer == 1:
                sp.wait(x_ready[b])
                dma(out_stream, d["out"].rearrange("b (t p) d -> b p t d", p=P)[b], X[:, QT * b:QT * b + QT, :])
            gathers_done[g] = [x_ready[b]]
            route_free[g] = [x_ready[b], *weights_free]

        out_stream = Stream(sem("out_stored"))

        def run(gen):
            for _ in gen:
                pass

        def chain_of(*gens):
            for g in gens:
                yield from g

        def stacks(layer, b):
            load_stacks(layer, b)
            yield

        first_prep, second_prep = prep(0, 0), prep(0, 1)
        next(first_prep)
        next(first_prep)
        set_values()
        set_zeros(0)
        next(second_prep)
        run(chain_of(first_prep, stacks(0, 0)))
        load_rest()
        set_zeros(1)
        set_ones(1)
        pe.wait(*stacks_set[0])
        weave(maxima(0, 0, 0), MAX_STEPS, (second_prep, PREP_STEPS[0], 0.0, 0.8))
        load_stacks(0, 1)
        pe.wait(*stacks_set[1])
        filled = fill_with_zeros()
        BEGUN = 9
        for layer in range(2):
            second_half = maxima(layer, 0, 1)
            for b in range(BATCHES):
                sides = []
                if b > 0:
                    sides.append((after(layer, b - 1), 8, 0.55, 1.0))
                sides.append((second_half, MAX_STEPS - BEGUN, 0.0, 0.3))
                if b + 1 < BATCHES:
                    sides.append((maxima(layer, b + 1, 0), MAX_STEPS, 0.3, 0.8))
                    second_half = maxima(layer, b + 1, 1)
                    sides.append((islice(second_half, BEGUN), BEGUN, 0.8, 1.0))
                if b + 2 < BATCHES:
                    sides.append((prep(layer, b + 2), PREP_STEPS[layer], 0.0, 0.8))
                if b > GB:
                    done = (b - GB - 1,) if b < BATCHES - 1 else (GB - 2, GB - 1)
                    sides.append((chain_of(*[scatter(layer, 0, x) for x in done]), len(done) * SCATTER_STEPS[layer], 0.0, 0.45 * len(done)))
                if layer == 1 and b < GB:
                    sides.append((combine(0, 1, b), QT, 0.0, 0.6))
                got_w = (load_layer0_expert, load_layer1_expert)[layer](b)
                weave(core(layer, b), CORE_STEPS, *sides)
            shared = []
            for s in expd.slots:
                shared += s.freed
            rings = (rows_in, rows_t, silu_a, w1_now[layer], hidden_t, rows_out)
            for r in rings:
                for s in r.slots:
                    s.freed = list(shared)
            weave(experts(layer, 0, got_w), SLOTS[layer] + BEHIND,
                  (chain_of(after(layer, BATCHES - 1), *[scatter(layer, 1, x) for x in range(GB)]),
                   6 + GB * SCATTER_STEPS[layer], 0.0, 0.9))
            sides = [(chain_of(*[combine(layer, 0, x) for x in range(GB)]), GB * SCATTER_STEPS[layer], 0.0, 0.3 + 0.6 * layer)]
            if layer == 0:
                sides.append((chain_of(prep(1, 0), stacks(1, 0)), PREP_STEPS[1] + 1, 0.25, 0.6))
                sides.append((chain_of(prep(1, 1), stacks(1, 1)), PREP_STEPS[1] + 1, 0.6, 1.0))
                sides.append((maxima(1, 0, 0), MAX_STEPS, 0.8, 1.0))
            weave(experts(layer, 1, got_w), SLOTS[layer] + BEHIND, *sides)
            if layer == 0:
                shared = []
                for r in rings:
                    for s in r.slots:
                        shared += s.freed
                for s in expd.slots:
                    s.freed = list(shared)
        run(chain_of(*[combine(1, 1, x) for x in range(GB)]))
        sp.wait(Landed(out_stream.sem, out_stream.sent))
        for s in out_streams + scatter_streams:
            sp.wait(Landed(s.sem, s.sent))

        for q in (pe, act, dve, pool, sp):
            q.count()

        block = ctx.enter_context(nc.Block())

        @block.sync
        def _(eng):
            sp.emit(eng)

        @block.scalar
        def _(eng):
            act.emit(eng)

        @block.vector
        def _(eng):
            dve.emit(eng)

        @block.gpsimd
        def _(eng):
            pool.emit(eng)

        @block.tensor
        def _(eng):
            pe.emit(eng)


def constants():
    import numpy as np
    c = np.zeros((P, C_ALL), np.float32)
    p = np.arange(P)
    c[:, C_ID:C_ID + P] = np.eye(P)
    masks = np.zeros((P, 2 * P), np.float32)
    masks[:, 0:P] = np.where(p[None, :] > p[:, None], NEG, 0.0)
    masks[:, P:2 * P] = p[:, None] < p[None, :]
    c[:, C_FIRST:C_FIRST + P] = p[None, :] % GT != 0
    c[:, C_ONE:C_ONE + EXPERTS] = 1.0
    c[:, C_RANK:C_RANK + EXPERTS] = EXPERTS - np.arange(EXPERTS)
    c[:, C_THR:C_THR + GT] = P * np.arange(GT)
    c[:, C_SLOT:C_SLOT + MAXSLOTS] = np.arange(MAXSLOTS)
    c[:, C_HALF:C_HALF + QT] = -0.5
    half = HD // 2
    pos = np.arange(SEQ, dtype=np.float32)[:, None]
    inv = (1.0 / 10000.0 ** (np.arange(half, dtype=np.float32) / half)).astype(np.float32)
    ang = (pos * inv[None, :]).astype(np.float32)
    sin, cos = np.sin(ang).T, np.cos(ang).T
    cos_t = np.tile(np.concatenate([cos, cos], 0), (HEADS, 1))
    sin_t = np.tile(np.concatenate([-sin, sin], 0), (HEADS, 1))
    return c, masks, np.ascontiguousarray(cos_t, np.float32), np.ascontiguousarray(sin_t, np.float32)


def kernel(**inputs):
    import numpy as np
    import concourse.bacc as bacc
    from concourse.bass_utils import run_bass_kernel_spmd as launch

    a = {k: np.asarray(v) for k, v in inputs.items()}
    swap = [h * HD + (x + HD // 2) % HD for h in range(HEADS) for x in range(HD)]
    c, masks, cos_t, sin_t = constants()
    arrays = {
        "x": a["L0_attn_x"], "consts": c, "masks": masks, "cos": cos_t, "sin": sin_t,
        "wq0": a["L0_attn_wq"].T, "wk0": a["L0_attn_wk"].T, "wv0": a["L0_attn_wv"].T, "wo0": a["L0_attn_wo"].T,
        "router0": a["L0_ffn_router_w"], "router_b0": a["L0_ffn_router_b"], "w1_0": a["L0_ffn_w1"], "w2_0": a["L0_ffn_w2"],
        "wq1": a["L1_attn_W_q"], "wq1_sw": a["L1_attn_W_q"][:, swap], "wo1": a["L1_attn_W_o"], "wdkv": a["L1_attn_W_dkv"],
        "wuk": a["L1_attn_W_uk"], "wuk_sw": a["L1_attn_W_uk"][:, swap], "wuv": a["L1_attn_W_uv"],
        "ln_gamma": a["L1_attn_ln_gamma"], "ln_beta": a["L1_attn_ln_beta"],
        "router1": a["L1_ffn_gate_w"].T, "router_b1": a["L1_ffn_gate_b"],
        "w1_1": a["L1_ffn_w1"], "b1_t": a["L1_ffn_b1"].reshape(EXPERTS, FCH, P).transpose(0, 2, 1), "w2_1": a["L1_ffn_w2"], "b2": a["L1_ffn_b2"],
    }
    arrays = {k: np.ascontiguousarray(v) for k, v in arrays.items()}
    nc = bacc.Bacc("TRN2", target_bir_lowering=False, num_devices=1, dynamic_dma_scratch_size=8192)
    d = {k: nc.dram_tensor(f"in_{k}", v.shape, mybir.dt.from_np(v.dtype), kind="ExternalInput").ap() for k, v in arrays.items()}
    d["out"] = nc.dram_tensor("out_0", (BATCHES, SEQ, DIM), F32, kind="ExternalOutput").ap()
    two_layers(nc, d)
    r = launch(nc, [{f"in_{k}": v for k, v in arrays.items()}], core_ids=[0])
    return r.results[0]["out_0"]
```
